# Optimizing a Trainium2 kernel written in Bass

```python
import numpy as np
import jax
import jax.numpy as jnp

def _softmax(x, axis=-1):
    return jax.nn.softmax(x, axis=axis)

def _gelu(x):
    return jax.nn.gelu(x, approximate=True)

def _silu(x):
    return jax.nn.silu(x)

def _sigmoid(x):
    return jax.nn.sigmoid(x)

def _layernorm(x, axis=-1, eps=1e-05):
    m = jnp.mean(x, axis=axis, keepdims=True)
    v = jnp.var(x, axis=axis, keepdims=True)
    return (x - m) / jnp.sqrt(v + eps)

def _scatter_add(tgt, idx, src, axis=0):
    return tgt.at[idx].add(src)

def _segment_sum(src, seg, n):
    return jax.ops.segment_sum(src, seg, n)
kernel_name = 'mk_lm_tower_d1_tok_ids1024_r4_e93a04'

def setup_inputs(seed: int=0):
    np.random.seed(seed)
    _w = jnp.asarray

    def _rec_inputs():
        import jax
        import jax.numpy as jnp
        _rk = jax.random.key(seed)
        x = jax.random.randint(jax.random.fold_in(_rk, 1), (64, 256), 0, 12564, jnp.int32)
        return x
    x = _rec_inputs()

    def _L0_tok_setup():
        import jax, jax.numpy as jnp
        import numpy as np
        VOCAB = 50257
        D_EMB = 64
        D_MODEL = 256
        key = jax.random.key(seed)
        k1, k2, k3 = jax.random.split(key, 3)
        x = jax.random.randint(k1, (8, 1024), 0, VOCAB, dtype=jnp.int64)
        emb_table = jax.random.normal(k2, (VOCAB, D_EMB), dtype=jnp.float32)
        bound = 1.0 / np.sqrt(D_EMB)
        proj_w = jax.random.uniform(k3, (D_MODEL, D_EMB), dtype=jnp.float32, minval=-bound, maxval=bound)
        return {'x': x, 'emb_table': emb_table, 'proj_w': proj_w}
    _L0_tok_all = _L0_tok_setup()
    _L0_tok_in = {k: v for k, v in _L0_tok_all.items() if k in ('emb_table', 'proj_w')}
    del _L0_tok_all

    def _L0_attn_setup():
        import jax, jax.numpy as jnp
        import numpy as np
        D_MODEL, STATE_DIM, CONV_K = (256, 64, 4)
        BATCH, SEQ = (2, 512)

        def _layernorm(x, g, b, eps=1e-05):
            mu = x.mean(-1, keepdims=True)
            var = ((x - mu) ** 2).mean(-1, keepdims=True)
            return (x - mu) * jax.lax.rsqrt(var + eps) * g + b
        key = jax.random.key(seed)
        ks = jax.random.split(key, 8)
        s = 0.02
        return {'x': jax.random.normal(ks[0], (BATCH, SEQ, D_MODEL), dtype=jnp.float32), 'ln_g': jnp.ones((D_MODEL,), jnp.float32), 'ln_b': jnp.zeros((D_MODEL,), jnp.float32), 'W_in': jax.random.normal(ks[1], (2 * D_MODEL, D_MODEL), jnp.float32) * s, 'conv_w': jax.random.normal(ks[2], (D_MODEL, 1, CONV_K), jnp.float32) * s, 'conv_b': jnp.zeros((D_MODEL,), jnp.float32), 'A_log': jnp.log(jnp.arange(1, STATE_DIM + 1, dtype=jnp.float32)), 'Dp': jnp.ones((D_MODEL,), jnp.float32), 'W_dt': jax.random.normal(ks[3], (D_MODEL, D_MODEL), jnp.float32) * s, 'b_dt': jnp.zeros((D_MODEL,), jnp.float32), 'W_B': jax.random.normal(ks[4], (STATE_DIM, D_MODEL), jnp.float32) * s, 'W_C': jax.random.normal(ks[5], (STATE_DIM, D_MODEL), jnp.float32) * s, 'W_out': jax.random.normal(ks[6], (D_MODEL, D_MODEL), jnp.float32) * s}
    _L0_attn_all = _L0_attn_setup()
    _L0_attn_in = {k: v for k, v in _L0_attn_all.items() if k in ('ln_g', 'ln_b', 'W_in', 'conv_w', 'conv_b', 'A_log', 'Dp', 'W_dt', 'b_dt', 'W_B', 'W_C', 'W_out')}
    del _L0_attn_all

    def _L0_ffn_setup():
        import jax, jax.numpy as jnp
        import numpy as np
        LORA_DIM = 16
        LORA_TOKEN_INDEX = 1
        B, S, D, H = (4, 512, 256, 1024)
        key = jax.random.key(seed)
        ks = jax.random.split(key, 6)
        x = jax.random.normal(ks[0], (B, S, D), dtype=jnp.float32)
        W1 = jax.random.normal(ks[1], (H, D), dtype=jnp.float32) * 0.02
        b1 = jnp.zeros((H,), dtype=jnp.float32)
        W2 = jax.random.normal(ks[2], (D, H), dtype=jnp.float32) * 0.02
        b2 = jnp.zeros((D,), dtype=jnp.float32)
        scale = jnp.asarray(0.001, dtype=jnp.float32)
        return {'x': x, 'W1': W1, 'b1': b1, 'W2': W2, 'b2': b2, 'scale': scale}
    _L0_ffn_all = _L0_ffn_setup()
    _L0_ffn_in = {k: v for k, v in _L0_ffn_all.items() if k in ('W1', 'b1', 'W2', 'b2', 'scale')}
    del _L0_ffn_all
    return {'x': x, 'L0_tok_emb_table': _L0_tok_in['emb_table'], 'L0_tok_proj_w': _L0_tok_in['proj_w'], 'L0_attn_ln_g': _L0_attn_in['ln_g'], 'L0_attn_ln_b': _L0_attn_in['ln_b'], 'L0_attn_W_in': _L0_attn_in['W_in'], 'L0_attn_conv_w': _L0_attn_in['conv_w'], 'L0_attn_conv_b': _L0_attn_in['conv_b'], 'L0_attn_A_log': _L0_attn_in['A_log'], 'L0_attn_Dp': _L0_attn_in['Dp'], 'L0_attn_W_dt': _L0_attn_in['W_dt'], 'L0_attn_b_dt': _L0_attn_in['b_dt'], 'L0_attn_W_B': _L0_attn_in['W_B'], 'L0_attn_W_C': _L0_attn_in['W_C'], 'L0_attn_W_out': _L0_attn_in['W_out'], 'L0_ffn_W1': _L0_ffn_in['W1'], 'L0_ffn_b1': _L0_ffn_in['b1'], 'L0_ffn_W2': _L0_ffn_in['W2'], 'L0_ffn_b2': _L0_ffn_in['b2'], 'L0_ffn_scale': _L0_ffn_in['scale']}

def reference(x, L0_tok_emb_table, L0_tok_proj_w, L0_attn_ln_g, L0_attn_ln_b, L0_attn_W_in, L0_attn_conv_w, L0_attn_conv_b, L0_attn_A_log, L0_attn_Dp, L0_attn_W_dt, L0_attn_b_dt, L0_attn_W_B, L0_attn_W_C, L0_attn_W_out, L0_ffn_W1, L0_ffn_b1, L0_ffn_W2, L0_ffn_b2, L0_ffn_scale):
    import jax
    import jax.numpy as jnp

    def _L0_tok_ref(x, emb_table, proj_w):
        import jax, jax.numpy as jnp
        import numpy as np
        VOCAB = 50257
        D_EMB = 64
        D_MODEL = 256
        e = emb_table[x]
        return jnp.einsum('bse,de->bsd', e, proj_w)

    def _L0_attn_ref(x, ln_g, ln_b, W_in, conv_w, conv_b, A_log, Dp, W_dt, b_dt, W_B, W_C, W_out):
        import jax, jax.numpy as jnp
        import numpy as np
        D_MODEL, STATE_DIM, CONV_K = (256, 64, 4)
        BATCH, SEQ = (2, 512)

        def _layernorm(x, g, b, eps=1e-05):
            mu = x.mean(-1, keepdims=True)
            var = ((x - mu) ** 2).mean(-1, keepdims=True)
            return (x - mu) * jax.lax.rsqrt(var + eps) * g + b
        residual = x
        xn = _layernorm(x, ln_g, ln_b)
        xz = jnp.einsum('bsd,ed->bse', xn, W_in)
        x_main, z = jnp.split(xz, 2, axis=-1)
        xc = jax.lax.conv_general_dilated(jnp.swapaxes(x_main, 1, 2), conv_w, window_strides=(1,), padding=[(CONV_K - 1, 0)], feature_group_count=D_MODEL, dimension_numbers=('NCH', 'OIH', 'NCH'))
        x_conv = jax.nn.silu(jnp.swapaxes(xc, 1, 2) + conv_b)
        A = -jnp.exp(A_log)
        dt = jax.nn.softplus(jnp.einsum('bsd,ed->bse', x_conv, W_dt) + b_dt)
        Bm = jnp.einsum('bsd,nd->bsn', x_conv, W_B)
        Cm = jnp.einsum('bsd,nd->bsn', x_conv, W_C)

        def step(h, inp):
            dt_t, xc_t, B_t, C_t = inp
            A_bar = jnp.exp(A * dt_t[..., None])
            h = A_bar * h + xc_t[..., None] * B_t[:, None, :]
            y_t = jnp.einsum('bdn,bn->bd', h, C_t) + xc_t * Dp
            return (h, y_t)
        h0 = jnp.zeros((x.shape[0], D_MODEL, STATE_DIM), x.dtype)
        xs = (jnp.swapaxes(dt, 0, 1), jnp.swapaxes(x_conv, 0, 1), jnp.swapaxes(Bm, 0, 1), jnp.swapaxes(Cm, 0, 1))
        _, ys = jax.lax.scan(step, h0, xs)
        y = jnp.swapaxes(ys, 0, 1) * jax.nn.silu(z)
        y = jnp.einsum('bsd,ed->bse', y, W_out)
        return y + residual

    def _L0_ffn_ref(x, W1, b1, W2, b2, scale):
        import jax, jax.numpy as jnp
        import numpy as np
        LORA_DIM = 16
        LORA_TOKEN_INDEX = 1
        B, S, D, H = (4, 512, 256, 1024)
        Bx, Sx, Dx = x.shape
        Hx = W1.shape[0]
        lt = jax.lax.dynamic_slice_in_dim(x, LORA_TOKEN_INDEX, LORA_DIM, axis=1)
        even = lt[:, ::2, :]
        odd = lt[:, 1::2, :]
        m1 = (even[:, :4, :, None] * odd[:, :4, None, :]).reshape(Bx, Hx, Dx)
        m2 = (even[:, 4:, :, None] * odd[:, 4:, None, :]).reshape(Bx, Dx, Hx)
        h = jnp.einsum('bsd,hd->bsh', x, W1) + scale * jnp.einsum('bsd,bhd->bsh', x, m1) + b1
        h = jax.nn.gelu(h, approximate=False)
        out = jnp.einsum('bsh,oh->bso', h, W2) + scale * jnp.einsum('bsh,boh->bso', h, m2) + b2
        return out
    h = _L0_tok_ref(x, L0_tok_emb_table, L0_tok_proj_w)
    h = h + _L0_attn_ref(_layernorm(h, axis=-1), L0_attn_ln_g, L0_attn_ln_b, L0_attn_W_in, L0_attn_conv_w, L0_attn_conv_b, L0_attn_A_log, L0_attn_Dp, L0_attn_W_dt, L0_attn_b_dt, L0_attn_W_B, L0_attn_W_C, L0_attn_W_out)
    h = h + _L0_ffn_ref(_layernorm(h, axis=-1), L0_ffn_W1, L0_ffn_b1, L0_ffn_W2, L0_ffn_b2, L0_ffn_scale)
    return h

_drawn_inputs = setup_inputs


def setup_inputs(seed=0):
    import zlib

    import numpy as np

    out = dict(_drawn_inputs(seed))
    spreads = {'L0_attn_ln_g': (1.0, 0.6),
     'L0_attn_ln_b': (0.0, 0.8),
     'L0_attn_conv_b': (0.0, 0.8),
     'L0_attn_Dp': (1.0, 0.6),
     'L0_attn_b_dt': (0.0, 0.8),
     'L0_ffn_b1': (0.0, 2.0),
     'L0_ffn_b2': (0.0, 2.0)}
    factors = {'L0_attn_W_in': 8.0,
     'L0_attn_conv_w': 8.0,
     'L0_attn_A_log': 8.0,
     'L0_attn_W_dt': 8.0,
     'L0_attn_W_B': 8.0,
     'L0_attn_W_C': 8.0,
     'L0_attn_W_out': 8.0,
     'L0_ffn_W1': 30.465,
     'L0_ffn_W2': 8.0}
    for name, (base, spread) in spreads.items():
        noise = np.random.default_rng([zlib.crc32(name.encode()), seed]).standard_normal(out[name].shape)
        drawn = base * np.exp(spread * noise) if base else spread * noise
        out[name] = jnp.asarray(drawn.astype(out[name].dtype))
    for name, factor in factors.items():
        out[name] = (out[name] * factor).astype(out[name].dtype)
    return out
```

```python
import concourse.bass as bass
from concourse import mybir
from contextlib import ExitStack

F32 = mybir.dt.float32
BF16 = mybir.dt.bfloat16
I32 = mybir.dt.int32
ALU = mybir.AluOpType
ACT = mybir.ActivationFunctionType

BATCH, SEQ, D, N, E, H = 64, 256, 256, 64, 64, 1024
G, NB = 2, 2
J, Q = 4, 16
TU = J * Q
UNITS_PER_GROUP = SEQ // TU
GROUPS = BATCH // (G * NB)
UNITS = GROUPS * UNITS_PER_GROUP
K2 = D // 128
HC = H // 128
TOK = G * 128
POS = 4
NPOS = TU // POS
TAPS = 4
EPS = 1e-5
X_PART = (0, 1, 0, 1, 2, 0)
B_PART = (0, 0, 1, 1, 0, 2)
NPROD = len(X_PART)
NROW = NB * (NPROD + 3)
RL_DMAS = J * NB * (NPROD + 3 + NPROD)
PACK = G * (2 * D + NB * N)
A_RING, H_RING = 4, 8
CSQ = 4
LORA_ROWS = 4 * G * NB

FRONT_STEPS = {
    "pe": ["embT", "h0", "xnT", "xm", "z", "dt", "bc", "xt"],
    "act": ["embT", "h0", "xnT", "xm", "silu_x", "silu_z", "e", "ln", "bc", "cs", "xt", "hi", "mid"],
    "dve": ["carry", "st1", "ag1", "xa", "st2", "ag2", "xn", "z", "cv0", "cv1", "cv2", "cv3",
            "dtx", "na", "dt"],
    "pool": ["ve1", "rs1", "hres", "ve2", "rs2", "w", "cw", "cc", "cl", "xd", "r1", "lo"],
}
BACK_STEPS = {
    "pe": ["yT", "wo", "hnT", "s", "hid0", "hid1", "hid2", "hid3", "q", "out"],
    "act": ["yT", "hnT", "hid0", "hid1", "hid2", "hid3", "gelu"],
    "dve": ["yadd", "h1", "st", "ag", "hn", "sm", "qm", "out"],
    "pool": ["ymul", "h1b", "ve", "rs"],
}


def build(nc, idx, table, proj, win, wdtb, wc2, wout, w1, w2, lng, lnb, convw, convb, alog,
          dp, bdt, b1, b2, scale, ident, sel, own, half, maskq, out):
    ctx = ExitStack()
    with ctx:
        def sb(name, shape, dt=F32):
            return ctx.enter_context(nc.sbuf_tensor(name, shape, dt))

        def sem(name):
            return ctx.enter_context(nc.semaphore(name))

        PROJ = sb("PROJ", [E, D])
        WIN = sb("WIN", [128, K2, 2 * D])
        WDTB = sb("WDTB", [128, K2, D + N])
        WC2 = sb("WC2", [128, K2, 128])
        WOUT = sb("WOUT", [128, K2, D])
        W1 = sb("W1", [128, K2, H])
        W2 = sb("W2", [128, HC, D])
        LNG = sb("LNG", [128, K2])
        LNB = sb("LNB", [128, K2])
        CONVW = sb("CONVW", [128, K2, TAPS])
        CONVB = sb("CONVB", [128, K2])
        ACOL = sb("ACOL", [128, 2])
        DPB = sb("DPB", [128, D])
        BDTB = sb("BDTB", [128, D])
        B1C = sb("B1C", [128, HC])
        B2B = sb("B2B", [128, D])
        SCL = sb("SCL", [128, 1])
        IDENT = sb("IDENT", [128, 128])
        HALF = sb("HALF", [128, NB])
        OWN = sb("OWN", [128, NB])
        SEL = sb("SEL", [128, 128], BF16)
        MASKQ = sb("MASKQ", [128, TOK])
        XBIAS = sb("XBIAS", [128, K2])
        ZBIAS = sb("ZBIAS", [128, D])
        NHALF = sb("NHALF", [128, G])
        IDX = sb("IDX", [128, 2 * UNITS_PER_GROUP], I32)
        EMB = sb("EMB", [128, G, E])
        EMBT = sb("EMBT", [E, TOK])
        H0 = sb("H0", [128, G, D])
        XA = sb("XA", [128, G, D])
        XN = XA
        ST = sb("ST", [128, 2, G, 6])
        MV = sb("MV", [128, 2, G, 2])
        VE = sb("VE", [128, 2, G])
        RS = sb("RS", [128, 2, G])
        XNT = sb("XNT", [128, K2, TOK])
        XM = sb("XM", [128, K2, G * NB, TAPS - 1 + TU])
        ZT = sb("ZT", [128, G, D])
        CV = [sb(f"CV{i}", [128, K2, G * NB, TU]) for i in range(2)]
        XCT = sb("XCT", [128, K2, TOK])
        DTX, DNA = H0, XA
        DEX, DW = (c[:, :, :, :].rearrange("p k s t -> p (k s t)").rearrange("p (g d) -> p g d", g=G)
                   for c in CV)
        PK = sb("PK", [128, PACK])
        PKX, PKDT = (PK[:, i * G * D:(i + 1) * G * D].rearrange("p (g d) -> p g d", g=G) for i in range(2))
        PKB = PK[:, 2 * G * D:].rearrange("p (g b n) -> p g b n", g=G, b=NB)
        HI = sb("HI", [128, PACK], BF16)
        MID = sb("MID", [128, PACK], BF16)
        LO = sb("LO", [128, PACK], BF16)
        HRES = sb("HRES", [128, UNITS_PER_GROUP, G, D])
        SZ = sb("SZ", [128, UNITS_PER_GROUP, G, D])
        XD = sb("XD", [128, UNITS_PER_GROUP, G, D])
        RM = sb("RM", [128, 2, Q, G, D], BF16)
        LS = sb("LS", [128, 2, Q, G, NB * N], BF16)
        CT = sb("CT", [128, 2, G, J, NB, Q])
        CS = sb("CS", [128, 2, G, J, CSQ, NB * Q])
        AR = sb("AR", [128, A_RING, G * D])
        HR = sb("HR", [128, H_RING, G * D])
        V = sb("V", [128, G * D])
        YG = sb("YG", [128, G, D])
        LNBW = YG[:, 0, :].rearrange("p (k c) -> p k c", k=K2)
        YM = sb("YM", [128, G, D])
        YT = sb("YT", [128, K2, TOK])
        H1 = sb("H1", [128, G, D])
        H1B = sb("H1B", [128, G, D])
        BST = sb("BST", [128, G, 6])
        BMV = sb("BMV", [128, G, 2])
        BVE = sb("BVE", [128, G])
        BRS = sb("BRS", [128, G])
        HN = sb("HN", [128, G, D])
        HNP = YM[:, :, :].rearrange("p g (r a) -> p g r a", r=4)
        HNT = YT
        O1 = sb("O1", [128, K2, LORA_ROWS])
        O2 = sb("O2", [128, K2, 32])
        E1 = sb("E1", [LORA_ROWS, H])
        E2 = sb("E2", [128, D])
        SM = sb("SM", [LORA_ROWS, TOK])
        HH = sb("HH", [128, HC, TOK])
        QM = sb("QM", [128, TOK])
        OUT = H1

        ps = [ctx.enter_context(nc.psum_tensor(n, [128, 512], F32))
              for n in ("DT0", "DT1", "U0", "U1", "Y", "FA", "FB", "BA")]
        DT, U, (Y, FA, FB, BA) = ps[0:2], ps[2:4], ps[4:8]

        weights_loaded = sem("weights_loaded")
        setup_dve = sem("setup_dve")
        setup_pe = sem("setup_pe")
        setup_act = sem("setup_act")
        setup_pool = sem("setup_pool")
        idx_loaded = sem("idx_loaded")
        emb_loaded = sem("emb_loaded")
        rl_loaded = [sem("rl_loaded_even"), sem("rl_loaded_odd")]
        lora_rows_loaded = sem("lora_rows_loaded")
        out_stored = sem("out_stored")
        dt_ready = sem("dt_ready")
        u_ready = sem("u_ready")
        a_ready = sem("a_ready")
        v_done = sem("v_done")
        h_done = sem("h_done")
        y_done = sem("y_done")
        cs_filled = sem("cs_filled")
        lora_cols = sem("lora_cols")
        lora_perm = sem("lora_perm")
        front_sem = {e: sem(f"front_{e}") for e in FRONT_STEPS}
        back_sem = {e: sem(f"back_{e}") for e in BACK_STEPS}
        waits_met = {e: sem(f"waits_met_{e}") for e in ("dve", "pool", "pe")}
        A_CREDIT, V_CREDIT, H_CREDIT, Y_CREDIT = 2, A_RING, 2, H_RING // POS

        def front_count(e, step, n):
            return n * len(FRONT_STEPS[e]) + FRONT_STEPS[e].index(step) + 1

        def back_count(e, step, m):
            return (m + 1) * len(BACK_STEPS[e]) + BACK_STEPS[e].index(step) + 1

        def rl_count(n, par):
            return (n - par + 2) * (RL_DMAS * 16 // 2)

        def stand(engine, me):
            engine.sem_inc(waits_met[me], 1)

        class Chain:

            def __init__(self, engine, me, sems, count, n, first=False):
                self.engine, self.me, self.sems, self.count, self.n, self.first = \
                    engine, me, sems, count, n, first

            def after(self, e, step):
                self.engine.wait_ge(self.sems[e], self.count(e, step, self.n))

            def after_previous(self, e, step):
                if not self.first:
                    self.engine.wait_ge(self.sems[e], self.count(e, step, self.n - 1))

            def done(self, instruction):
                instruction.then_inc(self.sems[self.me], 1)

        def front(engine, me, n, first=False):
            return Chain(engine, me, front_sem, front_count, n, first)

        def back(engine, me, m):
            return Chain(engine, me, back_sem, back_count, m)

        def by_token(ap):
            return ap.rearrange("p b (q j) -> p j b q", j=J)

        def lora_col(t):
            return t % J, t // J

        WEIGHT_LOADS = 22
        block = ctx.enter_context(nc.Block())

        @block.sync
        def _(sp):
            loads = [(PROJ, proj), (WIN, win), (WDTB, wdtb), (WC2, wc2), (WOUT, wout), (W1, w1), (W2, w2),
                     (LNG, lng), (LNB, lnb), (CONVW, convw), (CONVB, convb), (B1C, b1), (IDENT, ident),
                     (SEL, sel), (OWN, own), (HALF, half), (MASKQ, maskq)]
            for dst, src in loads:
                sp.dma_start(dst[:], src).then_inc(weights_loaded, 16)
            sp.dma_start(ACOL[:, 0:1], alog).then_inc(weights_loaded, 16)
            for dst, src in ((DPB, dp), (BDTB, bdt), (B2B, b2), (SCL, scale)):
                sp.dma_start(dst[:], src.to_broadcast(list(dst.shape))).then_inc(weights_loaded, 16)
            sp.wait_ge(setup_pool, 5)

            def spread_operands(n, par, first=False):
                front(sp, None, n, first).after("pool", "lo")
                parts = (HI, MID, LO)
                for j in range(J):
                    for b in range(NB):
                        tokens = slice(32 * j + Q * b, 32 * j + Q * b + Q)
                        for r in range(NPROD + 3):
                            part = parts[X_PART[r] if r < NPROD else r - NPROD]
                            lo = 0 if r < NPROD else G * D
                            row = 32 * j + NB * r + b
                            sp.dma_start(RM[row:row + 1, par].rearrange("p q g d -> p (q g d)"),
                                         part[tokens, lo:lo + G * D]).then_inc(rl_loaded[par], 16)
                            if r < NPROD:
                                sp.dma_start(LS[row:row + 1, par].rearrange("p q g n -> p (q g n)"),
                                             parts[B_PART[r]][tokens, 2 * G * D:]).then_inc(rl_loaded[par], 16)

            def lora_rows(grp):
                sp.wait_ge(lora_perm, grp + 1)
                for i in range(4):
                    for g in range(G):
                        row = 4 * i + NB * g
                        j, q = lora_col(1 + 2 * i)
                        p = 32 * j + q
                        sp.dma_start(E1[row:row + NB, i * D:(i + 1) * D],
                                     HN[p:p + Q + 1:Q, g, :]).then_inc(lora_rows_loaded, 16)
                        j, q = lora_col(9 + 2 * i)
                        p = 32 * j + q
                        for r in range(4):
                            sp.dma_start(E2[32 * r + row:32 * r + row + NB, i * N:(i + 1) * N],
                                         HNP[p:p + Q + 1:Q, g, r, :]).then_inc(lora_rows_loaded, 16)

            spread_operands(0, 0, first=True)
            with sp.Fori(0, GROUPS) as i:
                for tau in range(UNITS_PER_GROUP):
                    m = i * UNITS_PER_GROUP + tau
                    if tau == 1:
                        lora_rows(i)
                    spread_operands(m + 1, (tau + 1) % 2)
            sp.wait_ge(rl_loaded[0], rl_count(UNITS, 0))
            sp.wait_ge(out_stored, 16 * (UNITS + 2))

        @block.gpsimd
        def _(pool):
            for t in (LS, E1, E2, O2, CS):
                nc.gpsimd.memset(t[:], 0.0).then_inc(setup_pool, 1)
            nc.gpsimd.memset(NHALF[:], -0.5).then_inc(setup_pool, 1)
            for t in (HRES, SZ, XD):
                nc.gpsimd.memset(t[:, UNITS_PER_GROUP - 1], 0.0).then_inc(setup_pool, 1)
            pool.wait_ge(setup_pool, 9)
            nc.gpsimd.sem_inc(back_sem["pool"], len(BACK_STEPS["pool"]))
            pool.wait_ge(weights_loaded, WEIGHT_LOADS * 16)

            tt, ts = nc.gpsimd.tensor_tensor, nc.gpsimd.tensor_scalar

            def gather(n, col, first=False):
                c = front(pool, "pool", n, first)
                c.after_previous("pe", "embT")
                stand(pool, "pool")
                for g in range(G):
                    nc.gpsimd.indirect_dma_start(
                        out=EMB[:, g, :], out_offset=None, in_=table,
                        in_offset=bass.IndirectOffsetOnAxis(ap=IDX[:, col + g:col + g + 1], axis=0),
                    ).then_inc(emb_loaded, 16)

            def rstd1(n, u, first=False):
                c = front(pool, "pool", n, first)
                c.after("dve", "ag1")
                stand(pool, "pool")
                c.done(ts(VE[:, 0], MV[:, 0, :, 1], EPS, 1.0, ALU.add, ALU.mult))
                c.after("pool", "ve1")
                c.done(tt(RS[:, 0], VE[:, 0], NHALF[:], ALU.pow))

            def residual(n, u, first=False):
                c = front(pool, "pool", n, first)
                c.after("dve", "xa")
                c.done(tt(HRES[:, u], H0[:], XA[:], ALU.add))

            def rstd2(n, u, first=False):
                c = front(pool, "pool", n, first)
                c.after("dve", "ag2")
                stand(pool, "pool")
                c.done(ts(VE[:, 1], MV[:, 1, :, 1], EPS, 1.0, ALU.add, ALU.mult))
                c.after("pool", "ve2")
                c.done(tt(RS[:, 1], VE[:, 1], NHALF[:], ALU.pow))

            def softplus_w(n, u, first=False):
                c = front(pool, "pool", n, first)
                c.after("act", "e")
                stand(pool, "pool")
                c.done(ts(DW[:], DEX[:], 1.0, 1.0, ALU.add, ALU.mult))

            def softplus_fix(n, u, first=False):
                c = front(pool, "pool", n, first)
                c.after("act", "ln")
                stand(pool, "pool")
                c.done(ts(DW[:], DW[:], -1.0, 1.0, ALU.add, ALU.mult))
                c.after("pool", "cw")
                c.done(tt(DW[:], DEX[:], DW[:], ALU.subtract))
                c.after("pool", "cc")
                c.done(tt(DW[:], DNA[:], DW[:], ALU.add))

            def skip_x(n, u, first=False):
                c = front(pool, "pool", n, first)
                c.after("act", "xt")
                for g in range(G):
                    last = tt(XD[:, u, g], PKX[:, g], DPB[:], ALU.mult)
                c.done(last)

            def split_mid(n, u, first=False):
                c = front(pool, "pool", n, first)
                c.after("act", "hi")
                c.after("pool", "xd")
                c.done(tt(PK[:], PK[:], HI[:], ALU.subtract))

            def split_lo(n, u, par, first=False):
                c = front(pool, "pool", n, first)
                c.after("act", "mid")
                c.after("pool", "r1")
                c.done(tt(LO[:], PK[:], MID[:], ALU.subtract))

            def fill_cs(n, par, quarter, first=False):
                if quarter == 0:
                    front(pool, "pool", n, first).after("act", "cs")
                slot = quarter % 2
                if not first:
                    pool.wait_ge(y_done, Y_CREDIT + n * NPOS + (quarter - 1) * CSQ)
                    pool.wait_ge(cs_filled, n * (Q // CSQ) + quarter)
                stand(pool, "pool")
                q0 = quarter * CSQ
                for g in range(G):
                    def columns(first_q):
                        (pitch, parts), (per_j, js), (one, _) = CS[:, slot, g].rearrange("p j q c -> p j (q c)").ap
                        at = CS[:, slot, g, 0, 0, first_q:first_q + 1]
                        return bass.AP(tensor=at.tensor, offset=at.offset,
                                       ap=[[pitch, parts], [per_j, js], [Q, NB], [NB * Q + 1, CSQ]])

                    nc.gpsimd.memset(columns((q0 - 2 * CSQ) % Q), 0.0)
                    last = nc.gpsimd.tensor_copy(columns(q0), CT[:, par, g, :, :, q0:q0 + CSQ])
                last.then_inc(cs_filled, 1)

            def gate(m, u):
                c = back(pool, "pool", m)
                c.after("dve", "yadd")
                c.done(tt(YM[:], YG[:], SZ[:, u], ALU.mult))

            def add_b2(m, u):
                c = back(pool, "pool", m)
                c.after("dve", "h1")
                for g in range(G):
                    last = tt(H1B[:, g], H1[:, g], B2B[:], ALU.add)
                c.done(last)

            def rstd3(m, u):
                c = back(pool, "pool", m)
                c.after("dve", "ag")
                stand(pool, "pool")
                c.done(ts(BVE[:], BMV[:, :, 1], EPS, 1.0, ALU.add, ALU.mult))
                c.after("pool", "ve")
                c.done(tt(BRS[:], BVE[:], NHALF[:], ALU.pow))

            def lora_permute(m, grp):
                c = back(pool, "pool", m)
                c.after("dve", "hn")
                stand(pool, "pool")
                for g in range(G):
                    last = nc.gpsimd.tensor_copy(HNP[:, g], HN[:, g, :].rearrange("p (a r) -> p r a", r=4))
                last.then_inc(lora_perm, 1)

            FRONT = {3: [rstd1], 4: [residual, rstd2], 11: [softplus_w], 12: [softplus_fix, skip_x], 13: [split_mid]}
            BACK = {1: [gate], 3: [add_b2], 4: [rstd3]}

            def run_front(n, u, par, pos, first=False):
                for step in FRONT.get(pos, []):
                    step(n, u, first)
                if pos == 14:
                    split_lo(n, u, par, first)

            pool.dma_start(IDX[:], idx[0]).then_inc(idx_loaded, 16)
            pool.wait_ge(idx_loaded, 16)
            gather(0, 0, first=True)
            for pos in range(NPOS):
                run_front(0, 0, 0, pos, first=True)
            fill_cs(0, 0, 0, first=True)
            with pool.Fori(0, GROUPS) as i:
                pool.wait_ge(emb_loaded, i * (UNITS_PER_GROUP * G * 16) + 16 * G)
                pool.dma_start(IDX[:], idx[bass.ds(i + 1, 1)].rearrange("a p c -> (a p) c")).then_inc(idx_loaded, 16)
                pool.wait_ge(idx_loaded, i * 16 + 32)
                for tau in range(UNITS_PER_GROUP):
                    m = i * UNITS_PER_GROUP + tau
                    n, u, ub = m + 1, (tau + 1) % UNITS_PER_GROUP, (tau - 1) % UNITS_PER_GROUP
                    gather(n, G * tau)
                    for pos in range(NPOS):
                        for step in BACK.get(pos, []):
                            step(m, ub)
                        if tau == 1 and pos == 5:
                            lora_permute(m, i)
                        run_front(n, u, (tau + 1) % 2, pos)
                        if pos % CSQ == CSQ - 1 and pos < NPOS - 1:
                            fill_cs(m, tau % 2, pos // CSQ + 1)
                    fill_cs(n, (tau + 1) % 2, 0)
            for pos in range(NPOS):
                for step in BACK.get(pos, []):
                    step(UNITS, UNITS_PER_GROUP - 1)

        @block.scalar
        def _(act):
            f = nc.scalar.activation
            act.wait_ge(weights_loaded, WEIGHT_LOADS * 16)
            f(ACOL[:, 1:2], ACOL[:, 0:1], ACT.Exp).then_inc(setup_act, 1)
            act.wait_ge(setup_act, 1)
            f(ACOL[:, 0:1], ACOL[:, 1:2], ACT.Copy, scale=-1.0).then_inc(setup_act, 1)
            act.wait_ge(setup_act, 2)
            act.wait_ge(setup_pe, 2)
            f(XBIAS[:], FA[:, 0:K2], ACT.Copy).then_inc(setup_act, 1)
            f(ZBIAS[:], FB[:, 0:D], ACT.Copy).then_inc(setup_act, 1)
            act.wait_ge(setup_act, 4)
            nc.scalar.sem_inc(a_ready, A_CREDIT)
            nc.scalar.sem_inc(out_stored, 16)
            nc.scalar.sem_inc(back_sem["act"], len(BACK_STEPS["act"]))

            def embT(n, u, first=False):
                c = front(act, "act", n, first)
                c.after("pe", "embT")
                c.done(f(EMBT[:], FA[0:E, 0:TOK], ACT.Copy))

            def h0(n, u, first=False):
                c = front(act, "act", n, first)
                c.after("pe", "h0")
                c.after_previous("dve", "dt")
                c.done(f(H0[:], FB[:, :], ACT.Copy))

            def xnT(n, u, first=False):
                c = front(act, "act", n, first)
                c.after("pe", "xnT")
                c.done(f(XNT[:], FA[:, :], ACT.Copy))

            def xm(n, u, first=False):
                c = front(act, "act", n, first)
                c.after("pe", "xm")
                c.after("dve", "carry")
                for k in range(K2):
                    for g in range(G):
                        last = f(by_token(XM[:, k, NB * g:NB * g + NB, TAPS - 1:]),
                                 FB[:, k * TOK + g * 128:k * TOK + g * 128 + 128].rearrange(
                                     "p (j b q) -> p j b q", j=J, b=NB),
                                 ACT.Identity, bias=XBIAS[:, k:k + 1])
                c.done(last)

            def silu(n, u, first=False):
                c = front(act, "act", n, first)
                c.after("dve", "cv3")
                for k in range(K2):
                    for g in range(G):
                        last = f(XCT[:, k, g * 128:g * 128 + 128].rearrange("p (j b q) -> p j b q", j=J, b=NB),
                                 by_token(CV[1][:, k, NB * g:NB * g + NB, :]), ACT.Silu)
                c.done(last)
                c.done(f(SZ[:, u], ZT[:], ACT.Silu))

            def softplus_exp(n, u, first=False):
                c = front(act, "act", n, first)
                c.after("dve", "na")
                c.done(f(DEX[:], DNA[:], ACT.Exp))

            def softplus_ln(n, u, first=False):
                c = front(act, "act", n, first)
                c.after("pool", "w")
                c.after("act", "e")
                c.done(f(DNA[:], DW[:], ACT.Ln))

            def bc(n, u, par, first=False):
                c = front(act, "act", n, first)
                c.after("pe", "bc")
                c.after_previous("pool", "lo")
                for b in range(NB):
                    last = f(PKB[:, :, b, :], FA[:, 0:G * N].rearrange("p (g n) -> p g n", g=G), ACT.Identity,
                             scale=OWN[:, b:b + 1])
                c.done(last)
                for b in range(NB):
                    last = f(CT[:, par, :, :, b, :].rearrange("p g j q -> p (g j) q"),
                             FA[:, 128:128 + TOK].rearrange("p (x b q) -> p x b q", b=NB, q=Q)[:, :, b, :],
                             ACT.Identity, scale=HALF[:, b:b + 1])
                c.done(last)

            def xt(n, u, first=False):
                c = front(act, "act", n, first)
                c.after("pe", "xt")
                c.done(f(PK[:, 0:G * D], FB[:, :], ACT.Copy))

            def split_hi(n, u, par, first=False):
                c = front(act, "act", n, first)
                c.after("dve", "dt")
                c.after("act", "xt")
                if not first:
                    act.wait_ge(rl_loaded[1 - par], rl_count(n - 1, 1 - par))
                c.done(f(HI[:], PK[:], ACT.Copy))

            def split_mid(n, u, first=False):
                c = front(act, "act", n, first)
                c.after("pool", "r1")
                c.done(f(MID[:], PK[:], ACT.Copy))

            def yT(m, u):
                c = back(act, "act", m)
                c.after("pe", "yT")
                c.done(f(YT[:], BA[:, :], ACT.Copy))

            def hnT(m, u):
                c = back(act, "act", m)
                c.after("pe", "hnT")
                c.done(f(HNT[:], BA[:, :], ACT.Copy))

            def hidden(k):
                def step(m, u):
                    c = back(act, "act", m)
                    c.after("pe", f"hid{k}")
                    for h in range(2):
                        last = f(HH[:, 2 * k + h, :], BA[:, h * TOK:(h + 1) * TOK], ACT.Identity,
                                 bias=B1C[:, 2 * k + h:2 * k + h + 1])
                    c.done(last)
                return step

            def gelu(m, u):
                c = back(act, "act", m)
                c.after("act", "hid3")
                c.done(f(HH[:], HH[:], ACT.Gelu))

            def store(m, slot):
                c = back(act, "act", m)
                c.after("dve", "out")
                act.dma_start(slot, OUT[:, :, :]).then_inc(out_stored, 16)

            FRONT = {1: [embT], 2: [h0], 6: [xnT], 7: [xm], 9: [silu], 11: [softplus_exp, softplus_ln]}
            BACK = {2: [yT], 6: [hnT], 9: [hidden(0)], 10: [hidden(1)], 11: [hidden(2)], 12: [hidden(3), gelu]}

            def run_front(n, u, par, pos, first=False):
                for step in FRONT.get(pos, []):
                    step(n, u, first)
                if pos == 11:
                    bc(n, u, par, first)
                    xt(n, u, first)
                if pos == 13:
                    split_hi(n, u, par, first)
                    split_mid(n, u, first)

            def scan_step(m, t):
                T = m * TU + t
                act.wait_ge(dt_ready, T + 1)
                act.wait_ge(v_done, T + 1)
                f(AR[:, t % A_RING, :], DT[t % 2][:, :], ACT.Exp, scale=ACOL[:, 0:1]).then_inc(a_ready, 1)

            for pos in range(NPOS):
                run_front(0, 0, 0, pos, first=True)
            with act.Fori(0, GROUPS) as i:
                for tau in range(UNITS_PER_GROUP):
                    m = i * UNITS_PER_GROUP + tau
                    n, u, ub = m + 1, (tau + 1) % UNITS_PER_GROUP, (tau - 1) % UNITS_PER_GROUP
                    for pos in range(NPOS):
                        for t in range(pos * POS, (pos + 1) * POS):
                            scan_step(m, t)
                        for step in BACK.get(pos, []):
                            step(m, ub)
                        run_front(n, u, (tau + 1) % 2, pos)
                    store(m, out[bass.ds(m, 1)].rearrange("a p g d -> (a p) g d"))
            for pos in range(NPOS):
                for step in BACK.get(pos, []):
                    step(UNITS, UNITS_PER_GROUP - 1)
            store(UNITS, out[UNITS])

        @block.vector
        def _(dve):
            tt, ts, stt = nc.vector.tensor_tensor, nc.vector.tensor_scalar, nc.vector.scalar_tensor_tensor
            nc.vector.memset(V[:], 0.0).then_inc(setup_dve, 1)
            nc.vector.memset(HR[:], 0.0).then_inc(setup_dve, 1)
            nc.vector.memset(Y[:, :], 0.0).then_inc(setup_dve, 1)
            nc.vector.memset(O1[:], 0.0).then_inc(setup_dve, 1)
            nc.vector.memset(XM[:], 0.0).then_inc(setup_dve, 1)
            nc.vector.memset(LNBW, 1.0).then_inc(setup_dve, 1)
            dve.wait_ge(setup_dve, 6)
            dve.wait_ge(weights_loaded, WEIGHT_LOADS * 16)
            for k in range(K2):
                last = ts(LNBW[:, k, :], LNBW[:, k, :], LNB[:, k:k + 1], None, ALU.mult)
            last.then_inc(setup_dve, 1)
            dve.wait_ge(setup_pe, 2)
            for k in range(K2):
                last = ts(WIN[:, k, :], WIN[:, k, :], LNG[:, k:k + 1], None, ALU.mult)
            last.then_inc(setup_dve, 1)
            dve.wait_ge(setup_dve, 8)
            dve.wait_ge(setup_act, 4)
            dve.wait_ge(setup_pool, 9)
            nc.vector.sem_inc(v_done, V_CREDIT)
            nc.vector.sem_inc(h_done, H_CREDIT)
            nc.vector.sem_inc(back_sem["dve"], len(BACK_STEPS["dve"]))

            def carry(n, u, first=False):
                c = front(dve, "dve", n, first)
                c.after_previous("dve", "cv3")
                c.after_previous("act", "xm")
                if u == 0:
                    c.done(nc.vector.memset(XM[:, :, :, 0:TAPS - 1], 0.0))
                else:
                    c.done(nc.vector.tensor_copy(XM[:, :, :, 0:TAPS - 1], XM[:, :, :, TU:TU + TAPS - 1]))

            def stats(c, src, k, st, ag):
                for g in range(G):
                    last = nc.vector.bn_stats(ST[:, k, g, :], src[:, g, :])
                c.done(last)
                c.after("dve", st)
                stand(dve, "dve")
                for g in range(G):
                    last = nc.vector.bn_aggr(MV[:, k, g, :], ST[:, k, g, :])
                c.done(last)

            def stats1(n, u, first=False):
                c = front(dve, "dve", n, first)
                c.after("act", "h0")
                stats(c, H0, 0, "st1", "ag1")

            def norm1(n, u, first=False):
                c = front(dve, "dve", n, first)
                c.after("pool", "rs1")
                c.after_previous("pool", "cl")
                for g in range(G):
                    last = ts(XA[:, g], H0[:, g], MV[:, 0, g, 0:1], RS[:, 0, g:g + 1], ALU.subtract, ALU.mult)
                c.done(last)

            def stats2(n, u, first=False):
                c = front(dve, "dve", n, first)
                c.after("dve", "xa")
                stats(c, XA, 1, "st2", "ag2")

            def norm2(n, u, first=False):
                c = front(dve, "dve", n, first)
                c.after("pool", "rs2")
                c.after("pool", "hres")
                for g in range(G):
                    last = ts(XN[:, g], XA[:, g], MV[:, 1, g, 0:1], RS[:, 1, g:g + 1], ALU.subtract, ALU.mult)
                c.done(last)

            def z(n, u, first=False):
                c = front(dve, "dve", n, first)
                c.after("pe", "z")
                c.after_previous("act", "silu_z")
                for g in range(G):
                    last = tt(ZT[:, g], FA[:, g * D:(g + 1) * D], ZBIAS[:], ALU.add)
                c.done(last)

            def conv(n, u, first=False):
                c = front(dve, "dve", n, first)
                c.after("act", "xm")
                c.after_previous("dve", "dt")
                for tap in range(TAPS):
                    if tap:
                        c.after("dve", f"cv{tap - 1}")
                    at = TAPS - 1 - tap
                    for k in range(K2):
                        x = XM[:, k, :, at:at + TU]
                        if tap == 0:
                            last = ts(CV[0][:, k], x, CONVW[:, k, at:at + 1], CONVB[:, k:k + 1], ALU.mult, ALU.add)
                        else:
                            last = stt(CV[tap % 2][:, k], x, CONVW[:, k, at:at + 1], CV[1 - tap % 2][:, k],
                                       ALU.mult, ALU.add)
                    c.done(last)

            def dt_pre(n, u, first=False):
                c = front(dve, "dve", n, first)
                c.after("pe", "dt")
                for g in range(G):
                    last = tt(DTX[:, g], FB[:, g * D:(g + 1) * D], BDTB[:], ALU.add)
                c.done(last)
                c.after("dve", "dtx")
                c.done(stt(DNA[:], DTX[:], -1.0, DTX[:], ALU.mult, ALU.min))

            def dt_post(n, u, first=False):
                c = front(dve, "dve", n, first)
                c.after("pool", "cl")
                c.done(stt(PKDT, DTX[:], 0.0, DW[:], ALU.max, ALU.add))

            def y_add(m, u):
                c = back(dve, "dve", m)
                dve.wait_ge(y_done, Y_CREDIT + m * NPOS)
                c.done(tt(YG[:], Y[:, :].rearrange("p (g d) -> p g d", g=G), XD[:, u], ALU.add))

            def h1(m, u):
                c = back(dve, "dve", m)
                c.after("pe", "wo")
                dve.wait_ge(out_stored, (m + 1) * 16)
                c.done(tt(H1[:], BA[:, :].rearrange("p (g d) -> p g d", g=G), HRES[:, u], ALU.add))
                c.after("dve", "h1")
                for g in range(G):
                    last = nc.vector.bn_stats(BST[:, g, :], H1[:, g, :])
                c.done(last)
                c.after("dve", "st")
                stand(dve, "dve")
                for g in range(G):
                    last = nc.vector.bn_aggr(BMV[:, g, :], BST[:, g, :])
                c.done(last)

            def norm3(m, u):
                c = back(dve, "dve", m)
                c.after("pool", "rs")
                for g in range(G):
                    last = ts(HN[:, g], H1[:, g], BMV[:, g, 0:1], BRS[:, g:g + 1], ALU.subtract, ALU.mult)
                c.done(last)

            def lora_columns(m, grp):
                c = back(dve, "dve", m)
                c.after("act", "hnT")
                c.after_previous("pe", "q")
                for i in range(4):
                    for dst, t in ((O1, 2 + 2 * i), (O2, 10 + 2 * i)):
                        j, q = lora_col(t)
                        for k in range(K2):
                            last = nc.vector.tensor_copy(
                                dst[:, k, 4 * i:4 * i + 4].rearrange("p (g b) -> p g b", g=G),
                                HNT[:, k, :].rearrange("p (g j b q) -> p g j b q", g=G, j=J, b=NB)[:, :, j, :, q])
                last.then_inc(lora_cols, 1)

            def sm(m, u):
                c = back(dve, "dve", m)
                c.after("pe", "s")
                c.done(stt(SM[:], BA[0:LORA_ROWS, 0:TOK], SCL[0:LORA_ROWS, 0:1], MASKQ[0:LORA_ROWS, :], ALU.mult, ALU.mult))

            def qm(m, u):
                c = back(dve, "dve", m)
                c.after("pe", "q")
                c.done(stt(QM[:], BA[:, 0:TOK], SCL[:, 0:1], MASKQ[:], ALU.mult, ALU.mult))

            def out_add(m, u):
                c = back(dve, "dve", m)
                c.after("pe", "out")
                c.after("pool", "h1b")
                c.done(tt(OUT[:], BA[:, :].rearrange("p (g d) -> p g d", g=G), H1B[:], ALU.add))

            FRONT = {2: [carry], 3: [stats1], 4: [norm1, stats2], 5: [norm2], 8: [z, conv], 10: [dt_pre],
                     12: [dt_post]}
            BACK = {1: [y_add], 3: [h1], 5: [norm3], 8: [sm], 13: [qm], 15: [out_add]}

            def scan_step(m, t, fresh):
                T = m * TU + t
                dve.wait_ge(a_ready, A_CREDIT + T + 1)
                dve.wait_ge(h_done, H_CREDIT + T)
                if fresh:
                    nc.vector.memset(V[:], 0.0).then_inc(v_done, 1)
                else:
                    tt(V[:], AR[:, t % A_RING, :], HR[:, (t - 1) % H_RING, :], ALU.mult).then_inc(v_done, 1)
                dve.wait_ge(v_done, V_CREDIT + T + 1)
                dve.wait_ge(u_ready, T + 1)
                if t % POS == 0:
                    dve.wait_ge(y_done, m * NPOS + t // POS + 1)
                tt(HR[:, t % H_RING, :], V[:], U[t % 2][:, :], ALU.add).then_inc(h_done, 1)

            for pos in range(NPOS):
                for step in FRONT.get(pos, []):
                    step(0, 0, True)
            with dve.Fori(0, GROUPS) as i:
                for tau in range(UNITS_PER_GROUP):
                    m = i * UNITS_PER_GROUP + tau
                    n, u, ub = m + 1, (tau + 1) % UNITS_PER_GROUP, (tau - 1) % UNITS_PER_GROUP
                    for pos in range(NPOS):
                        if pos == 1:
                            y_add(m, ub)
                        for t in range(pos * POS, (pos + 1) * POS):
                            scan_step(m, t, tau == 0 and t == 0)
                        for step in BACK.get(pos, []):
                            if step is not y_add:
                                step(m, ub)
                        if tau == 1 and pos == 7:
                            lora_columns(m, i)
                        for step in FRONT.get(pos, []):
                            step(n, u)
            for pos in range(NPOS):
                for step in BACK.get(pos, []):
                    step(UNITS, UNITS_PER_GROUP - 1)

        @block.tensor
        def _(pe):
            mm = nc.tensor.matmul
            pe.wait_ge(weights_loaded, WEIGHT_LOADS * 16)
            for e in range(K2):
                for k in range(K2):
                    last = mm(FA[:, e:e + 1], WIN[:, k, e * 128:(e + 1) * 128], LNB[:, k:k + 1],
                              start=(k == 0), stop=(k == K2 - 1))
            last.then_inc(setup_pe, 1)
            pe.wait_ge(setup_dve, 7)
            for k in range(K2):
                last = mm(FB[:, 0:D], LNBW[:, k, :], WIN[:, k, D:2 * D], start=(k == 0), stop=(k == K2 - 1))
            last.then_inc(setup_pe, 1)
            pe.wait_ge(setup_dve, 8)
            pe.wait_ge(setup_act, 4)
            pe.wait_ge(setup_pool, 9)
            nc.tensor.sem_inc(y_done, Y_CREDIT)
            nc.tensor.sem_inc(back_sem["pe"], len(BACK_STEPS["pe"]))

            def embT(n, first=False):
                c = front(pe, "pe", n, first)
                pe.wait_ge(emb_loaded, (n + 1) * (16 * G))
                c.after_previous("act", "cs")
                stand(pe, "pe")
                for g in range(G):
                    last = nc.tensor.transpose(FA[0:E, g * 128:(g + 1) * 128], EMB[:, g, :], IDENT[:])
                c.done(last)

            def h0(n, first=False):
                c = front(pe, "pe", n, first)
                c.after("act", "embT")
                c.after_previous("act", "xt")
                for g in range(G):
                    last = mm(FB[:, g * D:(g + 1) * D], EMBT[:, g * 128:(g + 1) * 128], PROJ[:],
                              start=True, stop=True)
                c.done(last)

            def transposed(dst, src):
                for k in range(K2):
                    for g in range(G):
                        last = nc.tensor.transpose(dst[:, k * TOK + g * 128:k * TOK + (g + 1) * 128],
                                                   src[:, g, k * 128:(k + 1) * 128], IDENT[:])
                return last

            def xnT(n, first=False):
                c = front(pe, "pe", n, first)
                c.after("dve", "xn")
                c.after("act", "embT")
                c.done(transposed(FA, XN))

            def xm(n, first=False):
                c = front(pe, "pe", n, first)
                c.after("act", "xnT")
                c.after("act", "h0")
                for e in range(K2):
                    for k in range(K2):
                        last = mm(FB[:, e * TOK:(e + 1) * TOK], WIN[:, k, e * 128:(e + 1) * 128], XNT[:, k, :],
                                  start=(k == 0), stop=(k == K2 - 1))
                c.done(last)

            def by_tile(dst, width, lhs, rhs):
                for g in range(G):
                    for k in range(K2):
                        last = mm(dst[:, g * width:(g + 1) * width], lhs[:, k, g * 128:(g + 1) * 128], rhs[:, k],
                                  start=(k == 0), stop=(k == K2 - 1))
                return last

            def z(n, first=False):
                c = front(pe, "pe", n, first)
                c.after("act", "xnT")
                c.done(by_tile(FA, D, XNT, WIN[:, :, D:2 * D]))

            def dt(n, first=False):
                c = front(pe, "pe", n, first)
                c.after("act", "silu_x")
                c.after("act", "xm")
                c.done(by_tile(FB, D, XCT, WDTB[:, :, 0:D]))

            def bc(n, first=False):
                c = front(pe, "pe", n, first)
                c.after("act", "silu_x")
                c.after("dve", "z")
                by_tile(FA, N, XCT, WDTB[:, :, D:D + N])
                for k in range(K2):
                    last = mm(FA[:, 128:128 + TOK], WC2[:, k, :], XCT[:, k, :], start=(k == 0), stop=(k == K2 - 1))
                c.done(last)

            def xt(n, first=False):
                c = front(pe, "pe", n, first)
                c.after("dve", "dtx")
                for g in range(G):
                    for k in range(K2):
                        last = nc.tensor.transpose(FB[:, g * D + k * 128:g * D + (k + 1) * 128],
                                                   XCT[:, k, g * 128:(g + 1) * 128], IDENT[:])
                c.done(last)

            def yT(m):
                c = back(pe, "pe", m)
                c.after("pool", "ymul")
                c.after_previous("dve", "out")
                c.done(transposed(BA, YM))

            def wo(m):
                c = back(pe, "pe", m)
                c.after("act", "yT")
                c.done(by_tile(BA, D, YT, WOUT[:, :, :]))

            def hnT(m):
                c = back(pe, "pe", m)
                c.after("dve", "hn")
                c.done(transposed(BA, HN))

            def s(m, grp):
                c = back(pe, "pe", m)
                c.after("act", "hnT")
                pe.wait_ge(lora_cols, grp)
                for k in range(K2):
                    last = mm(BA[0:LORA_ROWS, 0:TOK], O1[:, k, :], HNT[:, k, :], start=(k == 0), stop=(k == K2 - 1))
                c.done(last)

            def hidden(k4, m, grp):
                c = back(pe, "pe", m)
                c.after("dve", "sm") if k4 == 0 else c.after("act", f"hid{k4 - 1}")
                if k4 == 0:
                    pe.wait_ge(lora_rows_loaded, grp * (4 * G * 5 * 16))
                    c.after_previous("pe", "out")
                for h in range(2):
                    col = (2 * k4 + h) * 128
                    for k in range(K2):
                        mm(BA[:, h * TOK:(h + 1) * TOK], W1[:, k, col:col + 128], HNT[:, k, :],
                           start=(k == 0), stop=False)
                    last = mm(BA[:, h * TOK:(h + 1) * TOK], E1[:, col:col + 128], SM[:], start=False, stop=True)
                c.done(last)

            def q(m):
                c = back(pe, "pe", m)
                c.after("act", "gelu")
                for k in range(K2):
                    for r in range(4):
                        last = mm(BA[32 * r:32 * r + 32, 0:TOK], O2[:, k, :], HH[:, K2 * r + k, :],
                                  start=(k == 0), stop=(k == K2 - 1), tile_position=(0, 32 * r))
                c.done(last)

            def out_mm(m):
                c = back(pe, "pe", m)
                c.after("dve", "qm")
                for g in range(G):
                    dst = BA[:, g * D:(g + 1) * D]
                    for h in range(HC):
                        mm(dst, HH[:, h, g * 128:(g + 1) * 128], W2[:, h, :], start=(h == 0), stop=False)
                    last = mm(dst, QM[:, g * 128:(g + 1) * 128], E2[:], start=False, stop=True)
                c.done(last)

            FRONT = {1: [embT], 2: [h0], 6: [xnT], 7: [xm, z], 10: [dt, bc], 11: [xt]}

            def run_back(m, grp, pos):
                if pos == 2:
                    yT(m)
                if pos == 3:
                    wo(m)
                if pos == 6:
                    hnT(m)
                if pos == 8:
                    s(m, grp)
                if 9 <= pos < 13:
                    hidden(pos - 9, m, grp)
                if pos == 13:
                    q(m)
                if pos == 14:
                    out_mm(m)

            def scan_in(m, par, t):
                T = m * TU + t
                j, qq = t % J, t // J
                rows = slice(32 * j, 32 * j + NROW)
                pe.wait_ge(a_ready, T + 1)
                for g in range(G):
                    last = mm(DT[t % 2][:, g * D:(g + 1) * D], SEL[rows, :], RM[rows, par, qq, g, :],
                              start=True, stop=True, tile_position=(32 * j, 0))
                last.then_inc(dt_ready, 1)
                pe.wait_ge(h_done, T + 1)
                for g in range(G):
                    last = mm(U[t % 2][:, g * D:(g + 1) * D], LS[rows, par, qq, g, :], RM[rows, par, qq, g, :],
                              start=True, stop=True, tile_position=(32 * j, 0))
                last.then_inc(u_ready, 1)

            def scan_out(m, pos, scanned):
                pe.wait_ge(h_done, H_CREDIT + scanned * TU + (pos + 1) * POS)
                if pos == 0:
                    pe.wait_ge(back_sem["dve"], back_count("dve", "yadd", m))
                if pos % CSQ == 0:
                    pe.wait_ge(cs_filled, scanned * (Q // CSQ) + pos // CSQ + 1)
                for g in range(G):
                    for j in range(J):
                        last = mm(Y[32 * j:32 * j + 32, g * D:(g + 1) * D], CS[:, pos // CSQ % 2, g, j, pos % CSQ, :],
                                  HR[:, (pos * POS + j) % H_RING, g * D:(g + 1) * D],
                                  start=(pos == 0 and g == 0), stop=(pos == NPOS - 1),
                                  tile_position=(0, 32 * j), skip_group_check=True)
                last.then_inc(y_done, 1)

            for pos in range(NPOS):
                for step in FRONT.get(pos, []):
                    step(0, True)
            with pe.Fori(0, GROUPS) as i:
                for tau in range(UNITS_PER_GROUP):
                    m = i * UNITS_PER_GROUP + tau
                    par = tau % 2
                    grp = i if tau == 0 else i + 1
                    pe.wait_ge(rl_loaded[par], rl_count(m, par))
                    for pos in range(NPOS):
                        for t in range(pos * POS, (pos + 1) * POS):
                            scan_in(m, par, t)
                            if t % POS == 1:
                                if pos:
                                    scan_out(m, pos - 1, m)
                                elif tau:
                                    scan_out(m, NPOS - 1, m - 1)
                        run_back(m, grp, pos)
                        for step in FRONT.get(pos, []):
                            step(m + 1)
                    if tau == UNITS_PER_GROUP - 1:
                        scan_out(m, NPOS - 1, m)
            for pos in range(NPOS):
                run_back(UNITS, GROUPS, pos)


def program(nc, args):
    build(nc, *args)


def kernel(x, L0_tok_emb_table, L0_tok_proj_w, L0_attn_ln_g, L0_attn_ln_b, L0_attn_W_in, L0_attn_conv_w,
           L0_attn_conv_b, L0_attn_A_log, L0_attn_Dp, L0_attn_W_dt, L0_attn_b_dt, L0_attn_W_B, L0_attn_W_C,
           L0_attn_W_out, L0_ffn_W1, L0_ffn_b1, L0_ffn_W2, L0_ffn_b2, L0_ffn_scale):
    import ml_dtypes
    import numpy as np
    import concourse.bacc as bacc
    from concourse.bass_utils import run_bass_kernel_spmd

    def arr(a):
        return np.ascontiguousarray(np.asarray(a))

    def by_rows(w):
        w = np.asarray(w)
        return arr(w.T.reshape(-1, 128, w.shape[0]).transpose(1, 0, 2))

    def by_cols(v):
        return arr(np.asarray(v).reshape(-1, 128).T)

    xi = np.asarray(x).reshape(GROUPS, G, NB, UNITS_PER_GROUP, Q, J).transpose(0, 3, 5, 2, 4, 1)
    xi = xi.reshape(UNITS, 128, G)
    idx = np.zeros((GROUPS + 1, 128, UNITS_PER_GROUP, G), xi.dtype)
    idx[0, :, 0] = xi[0]
    for i in range(GROUPS):
        for tau in range(UNITS_PER_GROUP):
            if i * UNITS_PER_GROUP + tau + 1 < UNITS:
                idx[i + 1, :, tau] = xi[i * UNITS_PER_GROUP + tau + 1]
    idx = idx.reshape(GROUPS + 1, 128, UNITS_PER_GROUP * G)

    sel = np.zeros((128, 128), ml_dtypes.bfloat16)
    for j in range(J):
        for r in range(NPROD, NPROD + 3):
            for b in range(NB):
                sel[32 * j + NB * r + b, N * b:N * b + N] = 1
    own = np.zeros((J, NB, Q, NB), np.float32)
    for b in range(NB):
        own[:, b, :, b] = 1
    half = np.repeat(np.eye(NB, dtype=np.float32), N, axis=0)
    mask16 = np.zeros((4, G, NB, G, J, NB, Q), np.float32)
    for g in range(G):
        for b in range(NB):
            mask16[:, g, b, g, :, b, :] = 1
    mask16 = mask16.reshape(LORA_ROWS, TOK)
    maskq = np.zeros((4, 32, TOK), np.float32)
    maskq[:, :LORA_ROWS] = mask16
    maskq = maskq.reshape(128, TOK)

    wc = np.asarray(L0_attn_W_C)
    alog = np.asarray(L0_attn_A_log)
    ins = {
        "idx": idx, "table": arr(L0_tok_emb_table), "proj": arr(np.asarray(L0_tok_proj_w).T),
        "win": by_rows(L0_attn_W_in),
        "wdtb": by_rows(np.concatenate([np.asarray(L0_attn_W_dt), np.asarray(L0_attn_W_B)])),
        "wc2": by_rows(np.concatenate([wc, wc])), "wout": by_rows(L0_attn_W_out),
        "w1": by_rows(L0_ffn_W1), "w2": by_rows(L0_ffn_W2),
        "lng": by_cols(L0_attn_ln_g), "lnb": by_cols(L0_attn_ln_b),
        "convw": arr(np.asarray(L0_attn_conv_w).reshape(K2, 128, TAPS).transpose(1, 0, 2)),
        "convb": by_cols(L0_attn_conv_b), "alog": arr(np.concatenate([alog, alog]).reshape(128, 1)),
        "dp": arr(L0_attn_Dp).reshape(1, D), "bdt": arr(L0_attn_b_dt).reshape(1, D),
        "b1": by_cols(L0_ffn_b1), "b2": arr(L0_ffn_b2).reshape(1, D),
        "scale": arr(L0_ffn_scale).reshape(1, 1),
        "ident": np.eye(128, dtype=np.float32), "sel": sel, "own": own.reshape(128, NB), "half": half, "maskq": maskq,
    }
    nc = bacc.Bacc("TRN2", target_bir_lowering=False, num_devices=1)
    args = [nc.dram_tensor(f"in_{k}", a.shape, mybir.dt.from_np(a.dtype), kind="ExternalInput").ap()
            for k, a in ins.items()]
    args.append(nc.dram_tensor("out", (UNITS + 1, 128, G, D), F32, kind="ExternalOutput").ap())
    program(nc, args)
    r = run_bass_kernel_spmd(nc, [{f"in_{k}": a for k, a in ins.items()}], core_ids=[0])
    o = r.results[0]["out"][1:].reshape(GROUPS, UNITS_PER_GROUP, J, NB, Q, G, D)
    return arr(o.transpose(0, 5, 3, 1, 4, 2, 6)).reshape(BATCH, SEQ, D)
```

```python
import concourse.bass as bass
from concourse import mybir
from contextlib import ExitStack

F32 = mybir.dt.float32
BF16 = mybir.dt.bfloat16
I32 = mybir.dt.int32
ALU = mybir.AluOpType
ACT = mybir.ActivationFunctionType

BATCH, SEQ, D, N, E, H = 64, 256, 256, 64, 64, 1024
G, NB = 4, 2
S = G * NB
HALVES = 2
PH = G // HALVES
T2, Q = 2, 16
TU = T2 * Q
UNITS_PER_GROUP = SEQ // TU
KEPT = 4
GROUPS = BATCH // S
UNITS = GROUPS * UNITS_PER_GROUP
K2 = D // 128
HC = H // 128
TOK = T2 * 128
QT = 8
QUARTERS = TU // QT
AHEAD = 2
TAPS = 4
EPS = 1e-5
X_PART = (0, 1, 0, 1, 2, 0)
B_PART = (0, 0, 1, 1, 0, 2)
NPROD = len(X_PART)
NROW = NB * (NPROD + 3)
XW, BW = T2 * D, T2 * NB * N
PACK = 2 * XW + BW
A_RING, H_RING = 4, 4
LORA_ROWS = 4 * S
WRITES = (NPROD + 3) + NPROD
READS = 2 * NB * QUARTERS
WEIGHT_LOADS = 22

FRONT_STEPS = {
    "pe": ["embT", "h0", "xnT", "xm", "z", "dt", "bc", "xt"],
    "act": ["embT", "h0", "xnT", "xm", "silu_x", "silu_z", "e", "ln", "bc", "cs", "xt", "hi", "mid"],
    "dve": ["carry", "st1", "ag1", "xa", "st2", "ag2", "xn", "z", "cv0", "cv1", "cv2", "cv3",
            "dtx", "na", "w", "wl", "dt"],
    "pool": ["ve1", "rs1", "hres", "ve2", "rs2", "cl", "xd", "r1", "lo"],
}
BACK_STEPS = {
    "pe": ["yT", "wo", "hnT", "s", "hid0", "hid1", "hid2", "hid3", "q", "out"],
    "act": ["yT", "hnT", "hid0", "hid1", "hid2", "hid3", "gelu"],
    "dve": ["yadd", "h1", "st", "ag", "hn", "sm", "qm", "out"],
    "pool": ["ymul", "ve", "rs", "h1b"],
}


def build(nc, idx, table, proj, win, wdtb, wc2, wout, w1, w2, lng, lnb, convw, convb, alog,
          dp, bdt, b1, b2, scale, ident, sel, own, half, maskq, xs, bs, out):
    ctx = ExitStack()
    with ctx:
        def sb(name, shape, dt=F32):
            return ctx.enter_context(nc.sbuf_tensor(name, shape, dt))

        def sem(name):
            return ctx.enter_context(nc.semaphore(name))

        PROJ = sb("PROJ", [E, D])
        WIN = sb("WIN", [128, K2, 2 * D])
        WDTB = sb("WDTB", [128, K2, D + N])
        WC2 = sb("WC2", [128, K2, 128])
        WOUT = sb("WOUT", [128, K2, D])
        W1 = sb("W1", [128, K2, H])
        W2 = sb("W2", [128, HC, D])
        LNG = sb("LNG", [128, K2])
        LNB = sb("LNB", [128, K2])
        CONVW = sb("CONVW", [128, K2, TAPS])
        CONVB = sb("CONVB", [128, K2])
        ACOL = sb("ACOL", [128, 2])
        DPB = sb("DPB", [128, D])
        BDTB = sb("BDTB", [128, D])
        B1C = sb("B1C", [128, HC])
        B2B = sb("B2B", [128, D])
        SCL = sb("SCL", [128, 1])
        IDENT = sb("IDENT", [128, 128])
        HALF = sb("HALF", [128, NB])
        OWN = sb("OWN", [128, NB])
        SEL = sb("SEL", [128, 128], BF16)
        MASKQ = sb("MASKQ", [128, TOK])
        XBIAS = sb("XBIAS", [128, K2])
        ZBIAS = sb("ZBIAS", [128, D])
        NHALF = sb("NHALF", [128, T2])
        IDX = sb("IDX", [128, T2 * UNITS_PER_GROUP], I32)
        EMB = sb("EMB", [128, T2, E])
        EMBT = sb("EMBT", [E, TOK])
        H0 = sb("H0", [128, T2, D])
        XA = sb("XA", [128, T2, D])
        XN = XA
        ST = sb("ST", [128, 2, T2, 6])
        MV = sb("MV", [128, 2, T2, 2])
        VE = sb("VE", [128, 2, T2])
        RS = sb("RS", [128, 2, T2])
        XNT = sb("XNT", [128, K2, TOK])
        XM = sb("XM", [128, K2, S, TAPS - 1 + TU])
        ZT = sb("ZT", [128, T2, D])
        CV = [sb(f"CV{i}", [128, K2, S, TU]) for i in range(2)]
        XCT = sb("XCT", [128, K2, TOK])
        DTX, DNA = H0, XA
        DEX, DW = (c[:, :, :, :].rearrange("p k s t -> p (k s t)").rearrange("p (h d) -> p h d", h=T2)
                   for c in CV)
        PK = sb("PK", [128, PACK])
        PKX, PKDT = (PK[:, i * XW:(i + 1) * XW].rearrange("p (h d) -> p h d", h=T2) for i in range(2))
        PKB = PK[:, 2 * XW:].rearrange("p (h b n) -> p h b n", h=T2, b=NB)
        HI = sb("HI", [128, PACK], BF16)
        MID = sb("MID", [128, PACK], BF16)
        LO = sb("LO", [128, PACK], BF16)
        HRES = sb("HRES", [128, KEPT, T2, D])
        SZ = sb("SZ", [128, KEPT, T2, D])
        XD = sb("XD", [128, KEPT, T2, D])
        RM = sb("RM", [128, 2, G, QT, D], BF16)
        LS = sb("LS", [128, 2, G, QT, NB * N], BF16)
        CT = sb("CT", [128, 2, T2, S, Q])
        CS = sb("CS", [128, 2, QT, G, NB * Q])
        AR = sb("AR", [128, A_RING, HALVES, PH * D])
        HR = sb("HR", [128, H_RING, HALVES, PH * D])
        V = sb("V", [128, HALVES, PH * D])
        YG = sb("YG", [128, T2, D])
        LNBW = YG[:, 0, :].rearrange("p (k c) -> p k c", k=K2)
        YM = sb("YM", [128, T2, D])
        YT = sb("YT", [128, K2, TOK])
        H1 = sb("H1", [128, T2, D])
        H1B = sb("H1B", [128, T2, D])
        BST = sb("BST", [128, T2, 6])
        BMV = sb("BMV", [128, T2, 2])
        BVE = sb("BVE", [128, T2])
        BRS = sb("BRS", [128, T2])
        HN = sb("HN", [128, T2, D])
        HNP = YM[:, :, :].rearrange("p h (r a) -> p h r a", r=4)
        HNT = YT
        O1 = sb("O1", [128, K2, LORA_ROWS])
        O2 = sb("O2", [128, K2, 32])
        E1 = sb("E1", [LORA_ROWS, H])
        E2 = sb("E2", [128, D])
        SM = sb("SM", [LORA_ROWS, TOK])
        HH = sb("HH", [128, HC, TOK])
        QM = YG[:, 0, :]
        OUT = H1

        ps = [ctx.enter_context(nc.psum_tensor(n, [128, 512], F32))
              for n in ("DT0", "DT1", "U0", "U1", "Y", "FA", "FB", "BA")]
        DT, U, (Y, FA, FB, BA) = ps[0:2], ps[2:4], ps[4:8]

        weights_loaded = sem("weights_loaded")
        setup_dve = sem("setup_dve")
        setup_pe = sem("setup_pe")
        setup_act = sem("setup_act")
        setup_pool = sem("setup_pool")
        idx_loaded = sem("idx_loaded")
        emb_loaded = sem("emb_loaded")
        rows_written = [sem("rows_written_even"), sem("rows_written_odd")]
        rl_loaded = [sem("rl_loaded_even"), sem("rl_loaded_odd")]
        lora_rows_loaded = sem("lora_rows_loaded")
        out_stored = sem("out_stored")
        dt_ready = sem("dt_ready")
        u_ready = sem("u_ready")
        a_ready = sem("a_ready")
        v_done = sem("v_done")
        h_done = sem("h_done")
        y_done = sem("y_done")
        cs_filled = sem("cs_filled")
        lora_cols = sem("lora_cols")
        lora_perm = sem("lora_perm")
        front_sem = {e: sem(f"front_{e}") for e in FRONT_STEPS}
        back_sem = {e: sem(f"back_{e}") for e in BACK_STEPS}
        waits_met = {e: sem(f"waits_met_{e}") for e in ("dve", "pool", "pe")}
        A_CREDIT, V_CREDIT, H_CREDIT, Y_CREDIT = HALVES, A_RING, HALVES, H_RING

        def front_count(e, step, n):
            return n * len(FRONT_STEPS[e]) + FRONT_STEPS[e].index(step) + 1

        def back_count(e, step, m):
            return (m + 1) * len(BACK_STEPS[e]) + BACK_STEPS[e].index(step) + 1

        def rl_count(n, par):
            return (n - par + 2) * (READS * 16 // 2)

        def stand(engine, me):
            engine.sem_inc(waits_met[me], 1)

        class Chain:

            def __init__(self, engine, me, sems, count, n, first=False):
                self.engine, self.me, self.sems, self.count, self.n, self.first = \
                    engine, me, sems, count, n, first

            def after(self, e, step):
                self.engine.wait_ge(self.sems[e], self.count(e, step, self.n))

            def after_previous(self, e, step):
                if not self.first:
                    self.engine.wait_ge(self.sems[e], self.count(e, step, self.n - 1))

            def done(self, instruction):
                instruction.then_inc(self.sems[self.me], 1)

        def front(engine, me, n, first=False):
            return Chain(engine, me, front_sem, front_count, n, first)

        def back(engine, me, m):
            return Chain(engine, me, back_sem, back_count, m)

        def by_token(ap):
            return ap.rearrange("p s (h q) -> p h s q", h=T2)

        def tiles(ap):
            return ap.rearrange("p (h d) -> p h d", h=T2)

        block = ctx.enter_context(nc.Block())

        @block.sync
        def _(sp):
            loads = [(PROJ, proj), (WIN, win), (WDTB, wdtb), (WC2, wc2), (WOUT, wout), (W1, w1), (W2, w2),
                     (LNG, lng), (LNB, lnb), (CONVW, convw), (CONVB, convb), (B1C, b1), (IDENT, ident),
                     (SEL, sel), (OWN, own), (HALF, half), (MASKQ, maskq)]
            for dst, src in loads:
                sp.dma_start(dst[:], src).then_inc(weights_loaded, 16)
            sp.dma_start(ACOL[:, 0:1], alog).then_inc(weights_loaded, 16)
            for dst, src in ((DPB, dp), (BDTB, bdt), (B2B, b2), (SCL, scale)):
                sp.dma_start(dst[:], src.to_broadcast(list(dst.shape))).then_inc(weights_loaded, 16)
            nc.sync.sem_inc(lora_rows_loaded, 16)
            sp.wait_ge(setup_pool, 5)

            def spread_operands(n, par, first=False):
                c = front(sp, None, n, first)
                for i, (part, e, step) in enumerate(((HI, "act", "hi"), (MID, "act", "mid"), (LO, "pool", "lo"))):
                    c.after(e, step)
                    for r in range(NPROD + 3):
                        if (X_PART[r] if r < NPROD else r - NPROD) == i:
                            lo = 0 if r < NPROD else XW
                            sp.dma_start(xs[par, r].rearrange("h p d -> p h d"),
                                         tiles(part[:, lo:lo + XW])).then_inc(rows_written[par], 16)
                        if r < NPROD and B_PART[r] == i:
                            sp.dma_start(bs[par, r].rearrange("h p c -> p h c"),
                                         tiles(part[:, 2 * XW:])).then_inc(rows_written[par], 16)
                sp.wait_ge(rows_written[par], (n - par + 2) * (WRITES * 16 // 2))
                for z in range(QUARTERS):
                    h, q0 = z * QT // Q, z * QT % Q
                    for b in range(NB):
                        row = 32 * z + (NPROD + 3) * b
                        x = xs[par, :, h].rearrange("r (g b q) d -> b r g q d", b=NB, q=Q)[b][:, :, q0:q0 + QT]
                        sp.dma_start(RM[row:row + NPROD + 3, par].rearrange("r g q d -> r g (q d)"),
                                     x.rearrange("r g q d -> r g (q d)")).then_inc(rl_loaded[par], 16)
                        x = bs[par, :, h].rearrange("r (g b q) d -> b r g q d", b=NB, q=Q)[b][:, :, q0:q0 + QT]
                        sp.dma_start(LS[row:row + NPROD, par].rearrange("r g q d -> r g (q d)"),
                                     x.rearrange("r g q d -> r g (q d)")).then_inc(rl_loaded[par], 16)

            def lora_rows(grp):
                sp.wait_ge(lora_perm, grp + 1)
                for i in range(4):
                    h, q = divmod(1 + 2 * i, Q)
                    sp.dma_start(E1[S * i:S * (i + 1), i * D:(i + 1) * D],
                                 HN[q:q + Q * (S - 1) + 1:Q, h, :]).then_inc(lora_rows_loaded, 16)
                    h, q = divmod(9 + 2 * i, Q)
                    for r in range(4):
                        row = LORA_ROWS * r + S * i
                        sp.dma_start(E2[row:row + S, i * N:(i + 1) * N],
                                     HNP[q:q + Q * (S - 1) + 1:Q, h, r, :]).then_inc(lora_rows_loaded, 16)

            spread_operands(0, 0, first=True)
            with sp.Fori(0, GROUPS) as i:
                for tau in range(UNITS_PER_GROUP):
                    m = i * UNITS_PER_GROUP + tau
                    if tau == 1:
                        lora_rows(i)
                    spread_operands(m + 1, (tau + 1) % 2)
            sp.wait_ge(rl_loaded[0], rl_count(UNITS, 0))
            sp.wait_ge(out_stored, 16 * (UNITS + 2))

        @block.gpsimd
        def _(pool):
            for t in (LS, E1, E2, O2, CS):
                nc.gpsimd.memset(t[:], 0.0).then_inc(setup_pool, 1)
            nc.gpsimd.memset(NHALF[:], -0.5).then_inc(setup_pool, 1)
            for t in (HRES, SZ, XD):
                nc.gpsimd.memset(t[:, KEPT - 1], 0.0).then_inc(setup_pool, 1)
            pool.wait_ge(setup_pool, 9)
            nc.gpsimd.sem_inc(back_sem["pool"], len(BACK_STEPS["pool"]))
            pool.wait_ge(weights_loaded, WEIGHT_LOADS * 16)

            tt, ts = nc.gpsimd.tensor_tensor, nc.gpsimd.tensor_scalar

            def gather(n, col, first=False):
                c = front(pool, "pool", n, first)
                c.after_previous("pe", "embT")
                stand(pool, "pool")
                for h in range(T2):
                    nc.gpsimd.indirect_dma_start(
                        out=EMB[:, h, :], out_offset=None, in_=table,
                        in_offset=bass.IndirectOffsetOnAxis(ap=IDX[:, col + h:col + h + 1], axis=0),
                    ).then_inc(emb_loaded, 16)

            def rstd1(n, u, first=False):
                c = front(pool, "pool", n, first)
                c.after("dve", "ag1")
                stand(pool, "pool")
                c.done(ts(VE[:, 0], MV[:, 0, :, 1], EPS, 1.0, ALU.add, ALU.mult))
                c.after("pool", "ve1")
                c.done(tt(RS[:, 0], VE[:, 0], NHALF[:], ALU.pow))

            def residual(n, u, first=False):
                c = front(pool, "pool", n, first)
                c.after("dve", "xa")
                c.done(tt(HRES[:, u % KEPT], H0[:], XA[:], ALU.add))

            def rstd2(n, u, first=False):
                c = front(pool, "pool", n, first)
                c.after("dve", "ag2")
                stand(pool, "pool")
                c.done(ts(VE[:, 1], MV[:, 1, :, 1], EPS, 1.0, ALU.add, ALU.mult))
                c.after("pool", "ve2")
                c.done(tt(RS[:, 1], VE[:, 1], NHALF[:], ALU.pow))

            def softplus_fix(n, u, first=False):
                c = front(pool, "pool", n, first)
                c.after("act", "ln")
                c.after("dve", "wl")
                c.done(tt(DW, DNA[:], DW, ALU.subtract))

            def skip_x(n, u, first=False):
                c = front(pool, "pool", n, first)
                c.after("act", "xt")
                for h in range(T2):
                    last = tt(XD[:, u % KEPT, h], PKX[:, h], DPB[:], ALU.mult)
                c.done(last)

            def split_mid(n, u, first=False):
                c = front(pool, "pool", n, first)
                c.after("act", "hi")
                c.after("pool", "xd")
                c.done(tt(PK[:], PK[:], HI[:], ALU.subtract))

            def split_lo(n, u, first=False):
                c = front(pool, "pool", n, first)
                c.after("act", "mid")
                c.after("pool", "r1")
                c.done(tt(LO[:], PK[:], MID[:], ALU.subtract))

            def fill_cs(n, par, z, first=False):
                if z == 0:
                    front(pool, "pool", n, first).after("act", "cs")
                if not first:
                    pool.wait_ge(y_done, Y_CREDIT + n * TU + (z - 1) * QT)
                    pool.wait_ge(cs_filled, n * QUARTERS + z)
                stand(pool, "pool")

                def columns(q):
                    at = CS[:, z % 2, 0, 0, q:q + 1]
                    return bass.AP(tensor=at.tensor, offset=at.offset,
                                   ap=[list(at.ap[0]), [Q, S], [G * NB * Q + 1, QT]])

                h, q0 = z * QT // Q, z * QT % Q
                last = nc.gpsimd.tensor_copy(columns(q0), CT[:, par, h, :, q0:q0 + QT])
                last.then_inc(cs_filled, 1)

            def gate(m, u):
                c = back(pool, "pool", m)
                c.after("dve", "yadd")
                c.done(tt(YM[:], YG[:], SZ[:, u % KEPT], ALU.mult))

            def add_b2(m, u):
                c = back(pool, "pool", m)
                c.after("dve", "h1")
                for h in range(T2):
                    last = tt(H1B[:, h], H1[:, h], B2B[:], ALU.add)
                c.done(last)

            def rstd3(m, u):
                c = back(pool, "pool", m)
                c.after("dve", "ag")
                stand(pool, "pool")
                c.done(ts(BVE[:], BMV[:, :, 1], EPS, 1.0, ALU.add, ALU.mult))
                c.after("pool", "ve")
                c.done(tt(BRS[:], BVE[:], NHALF[:], ALU.pow))

            def lora_permute(m, grp):
                c = back(pool, "pool", m)
                c.after("dve", "hn")
                stand(pool, "pool")
                for h in range(T2):
                    last = nc.gpsimd.tensor_copy(HNP[:, h], HN[:, h, :].rearrange("p (a r) -> p r a", r=4))
                last.then_inc(lora_perm, 1)

            FRONT = {3: [rstd1], 4: [residual, rstd2], 16: [softplus_fix, skip_x], 18: [split_mid], 20: [split_lo]}
            BACK = {1: [gate], 5: [rstd3], 6: [add_b2]}
            FILL = {3: 1, 11: 2, 19: 3, 27: 0}

            pool.dma_start(IDX[:], idx[0]).then_inc(idx_loaded, 16)
            pool.wait_ge(idx_loaded, 16)
            gather(0, 0, first=True)
            for t in range(TU):
                for step in FRONT.get(t, []):
                    step(0, 0, first=True)
            fill_cs(0, 0, 0, first=True)
            with pool.Fori(0, GROUPS) as i:
                pool.wait_ge(emb_loaded, i * (UNITS_PER_GROUP * T2 * 16) + 16 * T2)
                pool.dma_start(IDX[:], idx[bass.ds(i + 1, 1)].rearrange("a p c -> (a p) c")).then_inc(idx_loaded, 16)
                pool.wait_ge(idx_loaded, i * 16 + 32)
                for tau in range(UNITS_PER_GROUP):
                    m = i * UNITS_PER_GROUP + tau
                    n, u, ub = m + 1, tau + 1, tau - 1
                    gather(n, T2 * tau)
                    for t in range(TU):
                        for step in BACK.get(t, []):
                            step(m, ub)
                        if tau == 1 and t == 7:
                            lora_permute(m, i)
                        for step in FRONT.get(t, []):
                            step(n, u)
                        if t in FILL:
                            if FILL[t]:
                                fill_cs(m, tau % 2, FILL[t])
                            else:
                                fill_cs(n, (tau + 1) % 2, 0)
            for t in range(TU):
                for step in BACK.get(t, []):
                    step(UNITS, -1)

        @block.scalar
        def _(act):
            f = nc.scalar.activation
            act.wait_ge(weights_loaded, WEIGHT_LOADS * 16)
            f(ACOL[:, 1:2], ACOL[:, 0:1], ACT.Exp).then_inc(setup_act, 1)
            act.wait_ge(setup_act, 1)
            f(ACOL[:, 0:1], ACOL[:, 1:2], ACT.Copy, scale=-1.0).then_inc(setup_act, 1)
            act.wait_ge(setup_act, 2)
            act.wait_ge(setup_pe, 2)
            f(XBIAS[:], FA[:, 0:K2], ACT.Copy).then_inc(setup_act, 1)
            f(ZBIAS[:], FB[:, 0:D], ACT.Copy).then_inc(setup_act, 1)
            act.wait_ge(setup_act, 4)
            nc.scalar.sem_inc(a_ready, A_CREDIT)
            nc.scalar.sem_inc(out_stored, 16)
            nc.scalar.sem_inc(back_sem["act"], len(BACK_STEPS["act"]))

            def embT(n, u, first=False):
                c = front(act, "act", n, first)
                c.after("pe", "embT")
                c.done(f(EMBT[:], FA[0:E, 0:TOK], ACT.Copy))

            def h0(n, u, first=False):
                c = front(act, "act", n, first)
                c.after("pe", "h0")
                c.after_previous("dve", "dt")
                c.done(f(H0[:], FB[:, :], ACT.Copy))

            def xnT(n, u, first=False):
                c = front(act, "act", n, first)
                c.after("pe", "xnT")
                c.done(f(XNT[:], FA[:, :], ACT.Copy))

            def xm(n, u, first=False):
                c = front(act, "act", n, first)
                c.after("pe", "xm")
                c.after("dve", "carry")
                for k in range(K2):
                    last = f(by_token(XM[:, k, :, TAPS - 1:]),
                             FB[:, k * TOK:(k + 1) * TOK].rearrange("p (h s q) -> p h s q", h=T2, q=Q),
                             ACT.Identity, bias=XBIAS[:, k:k + 1])
                c.done(last)

            def silu(n, u, first=False):
                c = front(act, "act", n, first)
                c.after("dve", "cv3")
                for k in range(K2):
                    last = f(XCT[:, k, :].rearrange("p (h s q) -> p h s q", h=T2, q=Q),
                             by_token(CV[1][:, k]), ACT.Silu)
                c.done(last)
                c.done(f(SZ[:, u % KEPT], ZT[:], ACT.Silu))

            def softplus_exp(n, u, first=False):
                c = front(act, "act", n, first)
                c.after("dve", "na")
                c.done(f(DEX, DNA[:], ACT.Exp))

            def softplus_ln(n, u, first=False):
                c = front(act, "act", n, first)
                c.after("dve", "w")
                c.done(f(DNA[:], DW, ACT.Ln))

            def bc(n, u, par, first=False):
                c = front(act, "act", n, first)
                c.after("pe", "bc")
                c.after_previous("pool", "lo")
                for b in range(NB):
                    last = f(PKB[:, :, b, :], FA[:, 0:T2 * N].rearrange("p (h n) -> p h n", h=T2), ACT.Identity,
                             scale=OWN[:, b:b + 1])
                c.done(last)
                for b in range(NB):
                    last = f(CT[:, par].rearrange("p h (g b) q -> p (h g) b q", b=NB)[:, :, b, :],
                             FA[:, 128:128 + TOK].rearrange("p (x b q) -> p x b q", b=NB, q=Q)[:, :, b, :],
                             ACT.Identity, scale=HALF[:, b:b + 1])
                c.done(last)

            def xt(n, u, first=False):
                c = front(act, "act", n, first)
                c.after("pe", "xt")
                c.done(f(PK[:, 0:XW], FB[:, :], ACT.Copy))

            def split_hi(n, u, par, first=False):
                c = front(act, "act", n, first)
                c.after("dve", "dt")
                c.after("act", "xt")
                if not first:
                    act.wait_ge(rows_written[1 - par], (n - 1 - (1 - par) + 2) * (WRITES * 16 // 2))
                c.done(f(HI[:], PK[:], ACT.Copy))

            def split_mid(n, u, first=False):
                c = front(act, "act", n, first)
                c.after("pool", "r1")
                c.done(f(MID[:], PK[:], ACT.Copy))

            def yT(m, u):
                c = back(act, "act", m)
                c.after("pe", "yT")
                c.done(f(YT[:], BA[:, :], ACT.Copy))

            def hnT(m, u):
                c = back(act, "act", m)
                c.after("pe", "hnT")
                c.done(f(HNT[:], BA[:, :], ACT.Copy))

            def hidden(k):
                def step(m, u):
                    c = back(act, "act", m)
                    c.after("pe", f"hid{k}")
                    for h in range(2):
                        last = f(HH[:, 2 * k + h, :], BA[:, h * TOK:(h + 1) * TOK], ACT.Identity,
                                 bias=B1C[:, 2 * k + h:2 * k + h + 1])
                    c.done(last)
                return step

            def gelu(m, u):
                c = back(act, "act", m)
                c.after("act", "hid3")
                c.done(f(HH[:], HH[:], ACT.Gelu))

            def store(m, slot):
                c = back(act, "act", m)
                c.after("dve", "out")
                act.dma_start(slot, OUT[:, :, :]).then_inc(out_stored, 16)

            FRONT = {1: [embT], 2: [h0], 6: [xnT], 8: [xm], 11: [silu], 14: [softplus_exp],
                     15: [softplus_ln, bc, xt], 18: [split_hi], 20: [split_mid]}
            BACK = {3: [yT], 8: [hnT], 16: [hidden(0)], 18: [hidden(1)], 20: [hidden(2)], 22: [hidden(3), gelu]}
            BY_PARITY = (bc, split_hi)

            def run_front(n, u, par, t, first=False):
                for step in FRONT.get(t, []):
                    if step in BY_PARITY:
                        step(n, u, par, first)
                    else:
                        step(n, u, first)

            def scan_step(m, t):
                T = m * TU + t
                for e in range(HALVES):
                    act.wait_ge(dt_ready, HALVES * T + e + 1)
                    if e == 0:
                        act.wait_ge(v_done, T + 1)
                    f(AR[:, t % A_RING, e], DT[e][:, :], ACT.Exp, scale=ACOL[:, 0:1]).then_inc(a_ready, 1)

            for t in range(TU):
                run_front(0, 0, 0, t, first=True)
            with act.Fori(0, GROUPS) as i:
                for tau in range(UNITS_PER_GROUP):
                    m = i * UNITS_PER_GROUP + tau
                    n, u, ub = m + 1, tau + 1, tau - 1
                    for t in range(TU):
                        scan_step(m, t)
                        for step in BACK.get(t, []):
                            step(m, ub)
                        run_front(n, u, (tau + 1) % 2, t)
                    store(m, out[bass.ds(m, 1)].rearrange("a p h d -> (a p) h d"))
            scan_step(UNITS, 0)
            for t in range(TU):
                for step in BACK.get(t, []):
                    step(UNITS, -1)
            store(UNITS, out[UNITS])

        @block.vector
        def _(dve):
            tt, ts, stt = nc.vector.tensor_tensor, nc.vector.tensor_scalar, nc.vector.scalar_tensor_tensor
            nc.vector.memset(V[:], 0.0).then_inc(setup_dve, 1)
            nc.vector.memset(HR[:], 0.0).then_inc(setup_dve, 1)
            nc.vector.memset(Y[:, :], 0.0).then_inc(setup_dve, 1)
            nc.vector.memset(O1[:], 0.0).then_inc(setup_dve, 1)
            nc.vector.memset(XM[:], 0.0).then_inc(setup_dve, 1)
            nc.vector.memset(LNBW, 1.0).then_inc(setup_dve, 1)
            dve.wait_ge(setup_dve, 6)
            dve.wait_ge(weights_loaded, WEIGHT_LOADS * 16)
            for k in range(K2):
                last = ts(LNBW[:, k, :], LNBW[:, k, :], LNB[:, k:k + 1], None, ALU.mult)
            last.then_inc(setup_dve, 1)
            dve.wait_ge(setup_pe, 2)
            for k in range(K2):
                last = ts(WIN[:, k, :], WIN[:, k, :], LNG[:, k:k + 1], None, ALU.mult)
            last.then_inc(setup_dve, 1)
            dve.wait_ge(setup_dve, 8)
            dve.wait_ge(setup_act, 4)
            dve.wait_ge(setup_pool, 9)
            nc.vector.sem_inc(v_done, V_CREDIT)
            nc.vector.sem_inc(h_done, H_CREDIT)
            nc.vector.sem_inc(lora_cols, 1)
            nc.vector.sem_inc(back_sem["dve"], len(BACK_STEPS["dve"]))

            def carry(n, u, first=False):
                c = front(dve, "dve", n, first)
                c.after_previous("dve", "cv3")
                c.after_previous("act", "xm")
                if u % UNITS_PER_GROUP == 0:
                    c.done(nc.vector.memset(XM[:, :, :, 0:TAPS - 1], 0.0))
                else:
                    c.done(nc.vector.tensor_copy(XM[:, :, :, 0:TAPS - 1], XM[:, :, :, TU:TU + TAPS - 1]))

            def stats(c, src, k, st, ag):
                for h in range(T2):
                    last = nc.vector.bn_stats(ST[:, k, h, :], src[:, h, :])
                c.done(last)
                c.after("dve", st)
                stand(dve, "dve")
                for h in range(T2):
                    last = nc.vector.bn_aggr(MV[:, k, h, :], ST[:, k, h, :])
                c.done(last)

            def stats1(n, u, first=False):
                c = front(dve, "dve", n, first)
                c.after("act", "h0")
                stats(c, H0, 0, "st1", "ag1")

            def norm1(n, u, first=False):
                c = front(dve, "dve", n, first)
                c.after("pool", "rs1")
                c.after_previous("pool", "cl")
                for h in range(T2):
                    last = ts(XA[:, h], H0[:, h], MV[:, 0, h, 0:1], RS[:, 0, h:h + 1], ALU.subtract, ALU.mult)
                c.done(last)

            def stats2(n, u, first=False):
                c = front(dve, "dve", n, first)
                c.after("dve", "xa")
                stats(c, XA, 1, "st2", "ag2")

            def norm2(n, u, first=False):
                c = front(dve, "dve", n, first)
                c.after("pool", "rs2")
                c.after("pool", "hres")
                for h in range(T2):
                    last = ts(XN[:, h], XA[:, h], MV[:, 1, h, 0:1], RS[:, 1, h:h + 1], ALU.subtract, ALU.mult)
                c.done(last)

            def z(n, u, first=False):
                c = front(dve, "dve", n, first)
                c.after("pe", "z")
                c.after_previous("act", "silu_z")
                for h in range(T2):
                    last = tt(ZT[:, h], FA[:, h * D:(h + 1) * D], ZBIAS[:], ALU.add)
                c.done(last)

            def conv(n, u, first=False):
                c = front(dve, "dve", n, first)
                c.after("act", "xm")
                c.after_previous("dve", "dt")
                for tap in range(TAPS):
                    if tap:
                        c.after("dve", f"cv{tap - 1}")
                    at = TAPS - 1 - tap
                    for k in range(K2):
                        x = XM[:, k, :, at:at + TU]
                        if tap == 0:
                            last = ts(CV[0][:, k], x, CONVW[:, k, at:at + 1], CONVB[:, k:k + 1], ALU.mult, ALU.add)
                        else:
                            last = stt(CV[tap % 2][:, k], x, CONVW[:, k, at:at + 1], CV[1 - tap % 2][:, k],
                                       ALU.mult, ALU.add)
                    c.done(last)

            def dt_pre(n, u, first=False):
                c = front(dve, "dve", n, first)
                c.after("pe", "dt")
                for h in range(T2):
                    last = tt(DTX[:, h], FB[:, h * D:(h + 1) * D], BDTB[:], ALU.add)
                c.done(last)
                c.after("dve", "dtx")
                c.done(stt(DNA[:], DTX[:], -1.0, DTX[:], ALU.mult, ALU.min))

            def softplus_w(n, u, first=False):
                c = front(dve, "dve", n, first)
                c.after("act", "e")
                c.done(ts(DW, DEX, 1.0, None, ALU.add))

            def softplus_lost(n, u, first=False):
                c = front(dve, "dve", n, first)
                c.after("act", "ln")
                c.done(stt(DW, DW, 1.0, DEX, ALU.subtract, ALU.subtract))

            def dt_post(n, u, first=False):
                c = front(dve, "dve", n, first)
                c.after("pool", "cl")
                c.done(stt(PKDT, DTX[:], 0.0, DW, ALU.max, ALU.add))

            def y_add(m, u):
                c = back(dve, "dve", m)
                dve.wait_ge(y_done, Y_CREDIT + m * TU)
                c.done(tt(YG[:], tiles(Y[:, :]), XD[:, u % KEPT], ALU.add))

            def h1(m, u):
                c = back(dve, "dve", m)
                c.after("pe", "wo")
                dve.wait_ge(out_stored, (m + 1) * 16)
                c.done(tt(H1[:], tiles(BA[:, :]), HRES[:, u % KEPT], ALU.add))
                c.after("dve", "h1")
                for h in range(T2):
                    last = nc.vector.bn_stats(BST[:, h, :], H1[:, h, :])
                c.done(last)
                c.after("dve", "st")
                stand(dve, "dve")
                for h in range(T2):
                    last = nc.vector.bn_aggr(BMV[:, h, :], BST[:, h, :])
                c.done(last)

            def norm3(m, u):
                c = back(dve, "dve", m)
                c.after("pool", "rs")
                for h in range(T2):
                    last = ts(HN[:, h], H1[:, h], BMV[:, h, 0:1], BRS[:, h:h + 1], ALU.subtract, ALU.mult)
                c.done(last)

            def lora_columns(m, grp):
                c = back(dve, "dve", m)
                c.after("act", "hnT")
                c.after_previous("pe", "q")
                for i in range(4):
                    for dst, t in ((O1, 2 + 2 * i), (O2, 10 + 2 * i)):
                        h, q = divmod(t, Q)
                        last = nc.vector.tensor_copy(
                            dst[:, :, S * i:S * (i + 1)],
                            HNT[:, :, h * 128 + q:h * 128 + q + Q * (S - 1) + 1:Q])
                last.then_inc(lora_cols, 1)

            def sm(m, u):
                c = back(dve, "dve", m)
                c.after("pe", "s")
                c.done(stt(SM[:], BA[0:LORA_ROWS, 0:TOK], SCL[0:LORA_ROWS, 0:1], MASKQ[0:LORA_ROWS, :], ALU.mult, ALU.mult))

            def qm(m, u):
                c = back(dve, "dve", m)
                c.after("pe", "q")
                c.done(stt(QM, BA[:, 0:TOK], SCL[:, 0:1], MASKQ[:], ALU.mult, ALU.mult))

            def out_add(m, u):
                c = back(dve, "dve", m)
                c.after("pe", "out")
                c.after("pool", "h1b")
                c.done(tt(OUT[:], tiles(BA[:, :]), H1B[:], ALU.add))

            FRONT = {2: [carry], 3: [stats1], 4: [norm1, stats2], 5: [norm2], 9: [z], 10: [conv], 13: [dt_pre],
                     14: [softplus_w], 15: [softplus_lost], 17: [dt_post]}
            BACK = {0: [y_add], 5: [h1], 6: [norm3], 12: [sm], 25: [qm], 31: [out_add]}

            def scan_step(m, t, fresh):
                T = m * TU + t
                dve.wait_ge(a_ready, A_CREDIT + HALVES * (T + 1))
                dve.wait_ge(h_done, H_CREDIT + HALVES * T)
                if fresh:
                    nc.vector.memset(V[:], 0.0).then_inc(v_done, 1)
                else:
                    tt(V[:], AR[:, t % A_RING], HR[:, (t - 1) % H_RING], ALU.mult).then_inc(v_done, 1)
                dve.wait_ge(v_done, V_CREDIT + T + 1)
                dve.wait_ge(y_done, T + 1)
                for e in range(HALVES):
                    dve.wait_ge(u_ready, HALVES * T + e + 1)
                    tt(HR[:, t % H_RING, e], V[:, e], U[e][:, :], ALU.add).then_inc(h_done, 1)

            for t in range(TU):
                for step in FRONT.get(t, []):
                    step(0, 0, True)
            with dve.Fori(0, GROUPS) as i:
                for tau in range(UNITS_PER_GROUP):
                    m = i * UNITS_PER_GROUP + tau
                    n, u, ub = m + 1, tau + 1, tau - 1
                    for t in range(TU):
                        scan_step(m, t, tau == 0 and t == 0)
                        for step in BACK.get(t, []):
                            step(m, ub)
                        if tau == 1 and t == 10:
                            lora_columns(m, i)
                        for step in FRONT.get(t, []):
                            step(n, u)
            for t in range(TU):
                for step in BACK.get(t, []):
                    step(UNITS, -1)

        @block.tensor
        def _(pe):
            mm = nc.tensor.matmul
            pe.wait_ge(weights_loaded, WEIGHT_LOADS * 16)
            for e in range(K2):
                for k in range(K2):
                    last = mm(FA[:, e:e + 1], WIN[:, k, e * 128:(e + 1) * 128], LNB[:, k:k + 1],
                              start=(k == 0), stop=(k == K2 - 1))
            last.then_inc(setup_pe, 1)
            pe.wait_ge(setup_dve, 7)
            for k in range(K2):
                last = mm(FB[:, 0:D], LNBW[:, k, :], WIN[:, k, D:2 * D], start=(k == 0), stop=(k == K2 - 1))
            last.then_inc(setup_pe, 1)
            pe.wait_ge(setup_dve, 8)
            pe.wait_ge(setup_act, 4)
            pe.wait_ge(setup_pool, 9)
            nc.tensor.sem_inc(y_done, Y_CREDIT)
            nc.tensor.sem_inc(back_sem["pe"], len(BACK_STEPS["pe"]))

            def embT(n, first=False):
                c = front(pe, "pe", n, first)
                pe.wait_ge(emb_loaded, (n + 1) * (16 * T2))
                c.after_previous("act", "cs")
                stand(pe, "pe")
                for h in range(T2):
                    last = nc.tensor.transpose(FA[0:E, h * 128:(h + 1) * 128], EMB[:, h, :], IDENT[:])
                c.done(last)

            def h0(n, first=False):
                c = front(pe, "pe", n, first)
                c.after("act", "embT")
                c.after_previous("act", "xt")
                for h in range(T2):
                    last = mm(FB[:, h * D:(h + 1) * D], EMBT[:, h * 128:(h + 1) * 128], PROJ[:],
                              start=True, stop=True)
                c.done(last)

            def transposed(dst, src):
                for k in range(K2):
                    for h in range(T2):
                        last = nc.tensor.transpose(dst[:, k * TOK + h * 128:k * TOK + (h + 1) * 128],
                                                   src[:, h, k * 128:(k + 1) * 128], IDENT[:])
                return last

            def xnT(n, first=False):
                c = front(pe, "pe", n, first)
                c.after("dve", "xn")
                c.after("act", "embT")
                c.done(transposed(FA, XN))

            def xm(part):
                def step(n, first=False):
                    c = front(pe, "pe", n, first)
                    if part == 0:
                        c.after("act", "xnT")
                        c.after("act", "h0")
                    for k in range(K2):
                        last = mm(FB[:, part * TOK:(part + 1) * TOK], WIN[:, k, part * 128:(part + 1) * 128],
                                  XNT[:, k, :], start=(k == 0), stop=(k == K2 - 1))
                    if part == K2 - 1:
                        c.done(last)
                return step

            def tile_product(dst, width, h, lhs, rhs):
                for k in range(K2):
                    last = mm(dst[:, h * width:(h + 1) * width], lhs[:, k, h * 128:(h + 1) * 128], rhs[:, k],
                              start=(k == 0), stop=(k == K2 - 1))
                return last

            def z(h):
                def step(n, first=False):
                    c = front(pe, "pe", n, first)
                    if h == 0:
                        c.after("act", "xnT")
                    last = tile_product(FA, D, h, XNT, WIN[:, :, D:2 * D])
                    if h == T2 - 1:
                        c.done(last)
                return step

            def dt(h):
                def step(n, first=False):
                    c = front(pe, "pe", n, first)
                    if h == 0:
                        c.after("act", "silu_x")
                        c.after("act", "xm")
                    last = tile_product(FB, D, h, XCT, WDTB[:, :, 0:D])
                    if h == T2 - 1:
                        c.done(last)
                return step

            def bc(n, first=False):
                c = front(pe, "pe", n, first)
                c.after("act", "silu_x")
                c.after("dve", "z")
                for h in range(T2):
                    tile_product(FA, N, h, XCT, WDTB[:, :, D:D + N])
                for k in range(K2):
                    last = mm(FA[:, 128:128 + TOK], WC2[:, k, :], XCT[:, k, :], start=(k == 0), stop=(k == K2 - 1))
                c.done(last)

            def xt(n, first=False):
                c = front(pe, "pe", n, first)
                c.after("dve", "dtx")
                for h in range(T2):
                    for k in range(K2):
                        last = nc.tensor.transpose(FB[:, h * D + k * 128:h * D + (k + 1) * 128],
                                                   XCT[:, k, h * 128:(h + 1) * 128], IDENT[:])
                c.done(last)

            def yT(m, grp):
                c = back(pe, "pe", m)
                c.after("pool", "ymul")
                c.after_previous("dve", "out")
                c.done(transposed(BA, YM))

            def wo(h):
                def step(m, grp):
                    c = back(pe, "pe", m)
                    c.after("act", "yT")
                    last = tile_product(BA, D, h, YT, WOUT[:, :, :])
                    if h == T2 - 1:
                        c.done(last)
                return step

            def hnT(m, grp):
                c = back(pe, "pe", m)
                c.after("dve", "hn")
                c.done(transposed(BA, HN))

            def s(m, grp):
                c = back(pe, "pe", m)
                c.after("act", "hnT")
                pe.wait_ge(lora_cols, grp + 1)
                for k in range(K2):
                    last = mm(BA[0:LORA_ROWS, 0:TOK], O1[:, k, :], HNT[:, k, :], start=(k == 0), stop=(k == K2 - 1))
                c.done(last)

            def hidden(chunk):
                def step(m, grp):
                    c = back(pe, "pe", m)
                    half = chunk % 2
                    if chunk == 0:
                        c.after("dve", "sm")
                        pe.wait_ge(lora_rows_loaded, grp * (4 * 5 * 16) + 16)
                    elif half == 0:
                        c.after("act", f"hid{chunk // 2 - 1}")
                    dst, col = BA[:, half * TOK:(half + 1) * TOK], chunk * 128
                    for k in range(K2):
                        mm(dst, W1[:, k, col:col + 128], HNT[:, k, :], start=(k == 0), stop=False)
                    last = mm(dst, E1[:, col:col + 128], SM[:], start=False, stop=True)
                    if half:
                        c.done(last)
                return step

            def q(m, grp):
                c = back(pe, "pe", m)
                c.after("act", "gelu")
                for k in range(K2):
                    for r in range(4):
                        last = mm(BA[32 * r:32 * r + 32, 0:TOK], O2[:, k, :], HH[:, K2 * r + k, :],
                                  start=(k == 0), stop=(k == K2 - 1), tile_position=(0, 32 * r))
                c.done(last)

            def out_mm(h, part):
                def step(m, grp):
                    c = back(pe, "pe", m)
                    c.after("dve", "qm")
                    dst = BA[:, h * D:(h + 1) * D]
                    for k in range(part * HC // 2, (part + 1) * HC // 2):
                        mm(dst, HH[:, k, h * 128:(h + 1) * 128], W2[:, k, :], start=(k == 0), stop=False)
                    if part:
                        last = mm(dst, QM[:, h * 128:(h + 1) * 128], E2[:], start=False, stop=True)
                        if h == T2 - 1:
                            c.done(last)
                return step

            FRONT = {1: [embT], 2: [h0], 6: [xnT], 7: [xm(0)], 8: [xm(1)], 9: [z(0)], 10: [z(1)],
                     12: [dt(0)], 13: [dt(1), bc], 14: [xt]}
            BACK = {3: [yT], 4: [wo(0)], 5: [wo(1)], 8: [hnT], 11: [s], 25: [q], 26: [out_mm(0, 0)],
                    27: [out_mm(0, 1)], 28: [out_mm(1, 0)], 29: [out_mm(1, 1)]}
            BACK |= {15 + c: [hidden(c)] for c in range(HC)}

            def scan_dt(m, tau, t):
                T = m * TU + t
                par, local = (tau + t // TU) % 2, t % TU
                rows = slice(32 * (local // QT), 32 * (local // QT) + NROW)
                if local == 0:
                    pe.wait_ge(rl_loaded[par], rl_count(m + t // TU, par))
                for e in range(HALVES):
                    pe.wait_ge(a_ready, HALVES * T + e + 1)
                    for g in range(PH):
                        last = mm(DT[e][:, g * D:(g + 1) * D], SEL[rows, :], RM[rows, par, PH * e + g, local % QT, :],
                                  start=True, stop=True, tile_position=(rows.start, 0))
                    last.then_inc(dt_ready, 1)

            def scan_u(m, par, t):
                T = m * TU + t
                rows = slice(32 * (t // QT), 32 * (t // QT) + NROW)
                for e in range(HALVES):
                    pe.wait_ge(h_done, HALVES * T + e + 1)
                    for g in range(PH):
                        last = mm(U[e][:, g * D:(g + 1) * D], LS[rows, par, PH * e + g, t % QT, :],
                                  RM[rows, par, PH * e + g, t % QT, :],
                                  start=True, stop=True, tile_position=(rows.start, 0))
                    last.then_inc(u_ready, 1)

            def scan_y(m, t, slot):
                pe.wait_ge(h_done, H_CREDIT + HALVES * (m * TU + t + 1))
                if t == 0:
                    pe.wait_ge(back_sem["dve"], back_count("dve", "yadd", slot))
                if t % QT == 0:
                    pe.wait_ge(cs_filled, m * QUARTERS + t // QT + 1)
                h = t // Q
                for g in range(G):
                    last = mm(Y[32 * g:32 * g + 32, h * D:(h + 1) * D], CS[:, t // QT % 2, t % QT, g, :],
                              HR[:, t % H_RING, g // PH, g % PH * D:(g % PH + 1) * D],
                              start=(t == 0), stop=(t % Q == Q - 1),
                              tile_position=(0, 32 * g), skip_group_check=True)
                last.then_inc(y_done, 1)

            for t in range(TU):
                for step in FRONT.get(t, []):
                    step(0, True)
            for t in range(AHEAD):
                scan_dt(0, 0, t)
            with pe.Fori(0, GROUPS) as i:
                for tau in range(UNITS_PER_GROUP):
                    m = i * UNITS_PER_GROUP + tau
                    grp = i if tau == 0 else i + 1
                    for t in range(TU):
                        scan_u(m, tau % 2, t)
                        if t:
                            scan_y(m, t - 1, m)
                        elif tau:
                            scan_y(m - 1, TU - 1, m)
                        for step in BACK.get(t, []):
                            step(m, grp)
                        for step in FRONT.get(t, []):
                            step(m + 1)
                        scan_dt(m, tau, t + AHEAD)
                    if tau == UNITS_PER_GROUP - 1:
                        scan_y(m, TU - 1, m)
            for t in range(TU):
                for step in BACK.get(t, []):
                    step(UNITS, GROUPS)


def program(nc, args):
    build(nc, *args)


def kernel(x, L0_tok_emb_table, L0_tok_proj_w, L0_attn_ln_g, L0_attn_ln_b, L0_attn_W_in, L0_attn_conv_w,
           L0_attn_conv_b, L0_attn_A_log, L0_attn_Dp, L0_attn_W_dt, L0_attn_b_dt, L0_attn_W_B, L0_attn_W_C,
           L0_attn_W_out, L0_ffn_W1, L0_ffn_b1, L0_ffn_W2, L0_ffn_b2, L0_ffn_scale):
    import ml_dtypes
    import numpy as np
    import concourse.bacc as bacc
    from concourse.bass_utils import run_bass_kernel_spmd

    def arr(a):
        return np.ascontiguousarray(np.asarray(a))

    def by_rows(w):
        w = np.asarray(w)
        return arr(w.T.reshape(-1, 128, w.shape[0]).transpose(1, 0, 2))

    def by_cols(v):
        return arr(np.asarray(v).reshape(-1, 128).T)

    xi = np.asarray(x).reshape(GROUPS, S, UNITS_PER_GROUP, T2, Q).transpose(0, 2, 1, 4, 3)
    xi = xi.reshape(UNITS, 128, T2)
    idx = np.zeros((GROUPS + 1, 128, UNITS_PER_GROUP, T2), xi.dtype)
    idx[0, :, 0] = xi[0]
    for i in range(GROUPS):
        for tau in range(UNITS_PER_GROUP):
            if i * UNITS_PER_GROUP + tau + 1 < UNITS:
                idx[i + 1, :, tau] = xi[i * UNITS_PER_GROUP + tau + 1]
    idx = idx.reshape(GROUPS + 1, 128, UNITS_PER_GROUP * T2)

    sel = np.zeros((128, 128), ml_dtypes.bfloat16)
    for z in range(QUARTERS):
        for b in range(NB):
            row = 32 * z + (NPROD + 3) * b + NPROD
            sel[row:row + 3, N * b:N * b + N] = 1
    half = np.repeat(np.eye(NB, dtype=np.float32), N, axis=0)
    own = np.tile(np.repeat(np.eye(NB, dtype=np.float32), Q, axis=0), (G, 1))
    maskq = np.zeros((4 * 4, S, T2, S, Q), np.float32)
    for sq in range(S):
        maskq[:, sq, :, sq] = 1
    maskq = maskq.reshape(128, TOK)

    wc = np.asarray(L0_attn_W_C)
    alog = np.asarray(L0_attn_A_log)
    ins = {
        "idx": idx, "table": arr(L0_tok_emb_table), "proj": arr(np.asarray(L0_tok_proj_w).T),
        "win": by_rows(L0_attn_W_in),
        "wdtb": by_rows(np.concatenate([np.asarray(L0_attn_W_dt), np.asarray(L0_attn_W_B)])),
        "wc2": by_rows(np.concatenate([wc, wc])), "wout": by_rows(L0_attn_W_out),
        "w1": by_rows(L0_ffn_W1), "w2": by_rows(L0_ffn_W2),
        "lng": by_cols(L0_attn_ln_g), "lnb": by_cols(L0_attn_ln_b),
        "convw": arr(np.asarray(L0_attn_conv_w).reshape(K2, 128, TAPS).transpose(1, 0, 2)),
        "convb": by_cols(L0_attn_conv_b), "alog": arr(np.concatenate([alog, alog]).reshape(128, 1)),
        "dp": arr(L0_attn_Dp).reshape(1, D), "bdt": arr(L0_attn_b_dt).reshape(1, D),
        "b1": by_cols(L0_ffn_b1), "b2": arr(L0_ffn_b2).reshape(1, D),
        "scale": arr(L0_ffn_scale).reshape(1, 1),
        "ident": np.eye(128, dtype=np.float32), "sel": sel, "own": own, "half": half, "maskq": maskq,
    }
    nc = bacc.Bacc("TRN2", target_bir_lowering=False, num_devices=1)
    args = [nc.dram_tensor(f"in_{k}", a.shape, mybir.dt.from_np(a.dtype), kind="ExternalInput").ap()
            for k, a in ins.items()]
    args.append(nc.dram_tensor("rows_x", (2, NPROD + 3, T2, 128, D), BF16, kind="Internal").ap())
    args.append(nc.dram_tensor("rows_b", (2, NPROD, T2, 128, NB * N), BF16, kind="Internal").ap())
    args.append(nc.dram_tensor("out", (UNITS + 1, 128, T2, D), F32, kind="ExternalOutput").ap())
    program(nc, args)
    r = run_bass_kernel_spmd(nc, [{f"in_{k}": a for k, a in ins.items()}], core_ids=[0])
    o = r.results[0]["out"][1:].reshape(GROUPS, UNITS_PER_GROUP, S, Q, T2, D)
    return arr(o.transpose(0, 2, 1, 4, 3, 5)).reshape(BATCH, SEQ, D)
```

```python
import concourse.bass as bass
from concourse import mybir
from contextlib import ExitStack

F32 = mybir.dt.float32
BF16 = mybir.dt.bfloat16
I32 = mybir.dt.int32
ALU = mybir.AluOpType
ACT = mybir.ActivationFunctionType

BATCH, SEQ, D, N, E, H = 64, 256, 256, 64, 64, 1024
G, NB = 4, 2
S = G * NB
HALVES = 2
PH = G // HALVES
T2, Q = 2, 16
TU = T2 * Q
UNITS_PER_GROUP = SEQ // TU
KEPT = 4
GROUPS = BATCH // S
UNITS = GROUPS * UNITS_PER_GROUP
K2 = D // 128
HC = H // 128
TOK = T2 * 128
QT = 8
QUARTERS = TU // QT
AHEAD = 2
TAPS = 4
EPS = 1e-5
X_PART = (0, 1, 0, 1, 2, 0)
B_PART = (0, 0, 1, 1, 0, 2)
NPROD = len(X_PART)
NROW = NB * (NPROD + 3)
XW, BW = T2 * D, T2 * NB * N
XB = XW + BW
PACK = XB + XW
A_RING, H_RING = 4, 4
LORA_ROWS = 4 * S
WRITES = (NPROD + 3) + NPROD
READS = 2 * NB * QUARTERS
WEIGHT_LOADS = 22

EARLY_STEPS = {
    "pe": ["embT", "h0", "xnT"],
    "act": ["embT", "h0"],
    "dve": ["st1", "ag1", "st2", "ag2"],
    "pool": ["ve1", "rs1", "xa", "ve2", "rs2", "hres", "xn"],
}
LATE_STEPS = {
    "pe": ["xm", "z", "dt", "bc", "xt"],
    "act": ["xnT", "xm", "silu_x", "silu_z", "bc", "cs", "e", "xt", "hi_xb", "ln", "mid_xb", "hi_dt", "mid_dt"],
    "dve": ["carry", "cv0", "cv1", "cv2", "cv3", "z", "dtx", "na", "wl", "dt"],
    "pool": ["w", "xd", "r1_xb", "cl", "lo_xb", "r1_dt", "lo_dt"],
}
BACK_STEPS = {
    "pe": ["yT", "wo", "hnT", "s"] + [f"hid{c}" for c in range(HC)] + ["q", "out"],
    "act": ["yT", "hnT"] + [f"hid{c}" for c in range(HC)] + ["gelu"],
    "dve": ["yadd", "h1", "st", "ag", "sm", "qm", "out"],
    "pool": ["ymul", "ve", "rs", "hn", "h1b"],
}


def build(nc, idx, table, proj, win, wdtb, wc2, wout, w1, w2, lng, lnb, convw, convb, alog,
          dp, bdt, b1, b2, scale, ident, sel, own, half, maskq, xs, bs, out):
    ctx = ExitStack()
    with ctx:
        def sb(name, shape, dt=F32):
            return ctx.enter_context(nc.sbuf_tensor(name, shape, dt))

        def sem(name):
            return ctx.enter_context(nc.semaphore(name))

        PROJ = sb("PROJ", [E, D])
        WIN = sb("WIN", [128, K2, 2 * D])
        WDTB = sb("WDTB", [128, K2, D + N])
        WC2 = sb("WC2", [128, K2, 128])
        WOUT = sb("WOUT", [128, K2, D])
        W1 = sb("W1", [128, K2, H])
        W2 = sb("W2", [128, HC, D])
        LNG = sb("LNG", [128, K2])
        LNB = sb("LNB", [128, K2])
        CONVW = sb("CONVW", [128, K2, TAPS])
        CONVB = sb("CONVB", [128, K2])
        ACOL = sb("ACOL", [128, 2])
        DPB = sb("DPB", [128, D])
        BDTB = sb("BDTB", [128, D])
        B1C = sb("B1C", [128, HC])
        B2B = sb("B2B", [128, D])
        SCL = sb("SCL", [128, 1])
        IDENT = sb("IDENT", [128, 128])
        HALF = sb("HALF", [128, NB])
        OWN = sb("OWN", [128, NB])
        SEL = sb("SEL", [128, QUARTERS, 128], BF16)
        MASKQ = sb("MASKQ", [128, TOK])
        XBIAS = sb("XBIAS", [128, K2])
        ZBIAS = sb("ZBIAS", [128, D])
        NHALF = sb("NHALF", [128, T2])
        IDX = sb("IDX", [128, T2 * UNITS_PER_GROUP], I32)
        EMB = sb("EMB", [128, T2, E])
        H0 = sb("H0", [128, T2, D])
        XA = sb("XA", [128, T2, D])
        XN = XA
        ST = sb("ST", [128, 2, T2, 6])
        MV = sb("MV", [128, 2, T2, 2])
        VE = sb("VE", [128, 2, T2])
        RS = sb("RS", [128, 2, T2])
        XNT = sb("XNT", [128, K2, TOK])
        XM = sb("XM", [128, K2, S, TAPS - 1 + TU])
        ZT = sb("ZT", [128, T2, D])
        EMBT = ZT[0:E, 0, 0:TOK]
        CV = [sb(f"CV{i}", [128, K2, S, TU]) for i in range(2)]
        XCT = sb("XCT", [128, K2, TOK])
        DTX, DNA = H0, XA
        DEX, DW = (c[:, :, :, :].rearrange("p k s t -> p (k s t)").rearrange("p (h d) -> p h d", h=T2)
                   for c in CV)
        PK = sb("PK", [128, PACK])
        XB_COLS, DT_COLS = slice(0, XB), slice(XB, PACK)
        PKX, PKDT = (PK[:, c:c + XW].rearrange("p (h d) -> p h d", h=T2) for c in (0, XB))
        PKB = PK[:, XW:XB].rearrange("p (h b n) -> p h b n", h=T2, b=NB)
        HI = sb("HI", [128, PACK], BF16)
        MID = sb("MID", [128, PACK], BF16)
        LO = sb("LO", [128, PACK], BF16)
        HRES = sb("HRES", [128, KEPT, T2, D])
        SZ = sb("SZ", [128, KEPT, T2, D])
        XD = sb("XD", [128, KEPT, T2, D])
        RM = sb("RM", [128, 2, G, QT, D], BF16)
        LS = sb("LS", [128, 2, G, QT, NB * N], BF16)
        CT = sb("CT", [128, 2, T2, S, Q])
        CS = sb("CS", [128, 2, QT, G, NB * Q])
        AR = sb("AR", [128, A_RING, HALVES, PH * D])
        HR = sb("HR", [128, H_RING, HALVES, PH * D])
        V = sb("V", [128, HALVES, PH * D])
        YG = sb("YG", [128, T2, D])
        LNBW = YG[:, 0, :].rearrange("p (k c) -> p k c", k=K2)
        YM = sb("YM", [128, T2, D])
        YT = sb("YT", [128, K2, TOK])
        H1 = sb("H1", [128, T2, D])
        H1B = sb("H1B", [128, T2, D])
        BST = sb("BST", [128, T2, 6])
        BMV = sb("BMV", [128, T2, 2])
        BVE = sb("BVE", [128, T2])
        BRS = sb("BRS", [128, T2])
        HN = sb("HN", [128, T2, D])
        HNP = YM[:, :, :].rearrange("p h (r a) -> p h r a", r=4)
        HNT = YT
        O1 = sb("O1", [128, K2, LORA_ROWS])
        O2 = sb("O2", [128, K2, 32])
        E1 = sb("E1", [LORA_ROWS, H])
        E2 = sb("E2", [128, D])
        SM = sb("SM", [LORA_ROWS, TOK])
        HH = sb("HH", [128, HC, TOK])
        QM = YG[:, 0, :]
        OUT = H1

        ps = [ctx.enter_context(nc.psum_tensor(n, [128, 512], F32))
              for n in ("DT0", "DT1", "U0", "U1", "Y", "FA", "FB", "BA")]
        DT, U, (Y, FA, FB, BA) = ps[0:2], ps[2:4], ps[4:8]

        weights_loaded = sem("weights_loaded")
        setup_dve = sem("setup_dve")
        setup_pe = sem("setup_pe")
        setup_act = sem("setup_act")
        setup_pool = sem("setup_pool")
        idx_loaded = sem("idx_loaded")
        emb_loaded = sem("emb_loaded")
        rows_written = [sem("rows_written_even"), sem("rows_written_odd")]
        rl_loaded = [sem("rl_loaded_even"), sem("rl_loaded_odd")]
        lora_rows_loaded = sem("lora_rows_loaded")
        out_stored = sem("out_stored")
        dt_ready = sem("dt_ready")
        u_ready = sem("u_ready")
        a_ready = sem("a_ready")
        v_done = sem("v_done")
        h_done = sem("h_done")
        y_done = sem("y_done")
        cs_filled = sem("cs_filled")
        lora_cols = sem("lora_cols")
        lora_perm = sem("lora_perm")
        early_sem = {e: sem(f"early_{e}") for e in EARLY_STEPS}
        late_sem = {e: sem(f"late_{e}") for e in LATE_STEPS}
        back_sem = {e: sem(f"back_{e}") for e in BACK_STEPS}
        waits_met = {e: sem(f"waits_met_{e}") for e in ("dve", "pool", "pe")}
        A_CREDIT, V_CREDIT, H_CREDIT, Y_CREDIT = HALVES, HALVES * A_RING, HALVES, H_RING

        def back_count(e, step, m):
            return (m + 1) * len(BACK_STEPS[e]) + BACK_STEPS[e].index(step) + 1

        def rl_count(n, par):
            return (n - par + 2) * (READS * 16 // 2)

        def stand(engine, me):
            engine.sem_inc(waits_met[me], 1)

        class Front:

            def __init__(self, engine, me, n, first=False, early=False):
                self.engine, self.n, self.first = engine, n, first
                self.mine = (early_sem if early else late_sem).get(me)

            def after(self, e, step, before=0):
                sems, steps = (early_sem, EARLY_STEPS) if step in EARLY_STEPS[e] else (late_sem, LATE_STEPS)
                self.engine.wait_ge(sems[e], (self.n - before) * len(steps[e]) + steps[e].index(step) + 1)

            def after_previous(self, e, step):
                if not self.first:
                    self.after(e, step, before=1)

            def done(self, instruction):
                instruction.then_inc(self.mine, 1)

        class Back:

            def __init__(self, engine, me, m):
                self.engine, self.me, self.m = engine, me, m

            def after(self, e, step):
                self.engine.wait_ge(back_sem[e], back_count(e, step, self.m))

            def after_previous(self, e, step):
                self.engine.wait_ge(back_sem[e], back_count(e, step, self.m - 1))

            def done(self, instruction):
                instruction.then_inc(back_sem[self.me], 1)

        def early(engine, me, n, first=False):
            return Front(engine, me, n, first, early=True)

        def late(engine, me, n, first=False):
            return Front(engine, me, n, first)

        def back(engine, me, m):
            return Back(engine, me, m)

        def by_token(ap):
            return ap.rearrange("p s (h q) -> p h s q", h=T2)

        def tiles(ap):
            return ap.rearrange("p (h d) -> p h d", h=T2)

        block = ctx.enter_context(nc.Block())

        @block.sync
        def _(sp):
            loads = [(PROJ, proj), (WIN, win), (WDTB, wdtb), (WC2, wc2), (WOUT, wout), (W1, w1), (W2, w2),
                     (LNG, lng), (LNB, lnb), (CONVW, convw), (CONVB, convb), (B1C, b1), (IDENT, ident),
                     (SEL, sel), (OWN, own), (HALF, half), (MASKQ, maskq)]
            for dst, src in loads:
                sp.dma_start(dst[:], src).then_inc(weights_loaded, 16)
            sp.dma_start(ACOL[:, 0:1], alog).then_inc(weights_loaded, 16)
            for dst, src in ((DPB, dp), (BDTB, bdt), (B2B, b2), (SCL, scale)):
                sp.dma_start(dst[:], src.to_broadcast(list(dst.shape))).then_inc(weights_loaded, 16)
            nc.sync.sem_inc(lora_rows_loaded, 16)
            sp.wait_ge(setup_pool, 5)
            sp.wait_ge(setup_dve, 1)

            parts_xb = ((HI, "act", "hi_xb"), (MID, "act", "mid_xb"), (LO, "pool", "lo_xb"))
            parts_dt = ((HI, "act", "hi_dt"), (MID, "act", "mid_dt"), (LO, "pool", "lo_dt"))

            def spread_operands(n, par, first=False):
                c = late(sp, None, n, first)
                for i, (part, e, step) in enumerate(parts_xb):
                    c.after(e, step)
                    for r in range(NPROD):
                        if X_PART[r] == i:
                            sp.dma_start(xs[par, r].rearrange("h p d -> p h d"),
                                         tiles(part[:, 0:XW])).then_inc(rows_written[par], 16)
                        if B_PART[r] == i:
                            sp.dma_start(bs[par, r].rearrange("h p c -> p h c"),
                                         tiles(part[:, XW:XB])).then_inc(rows_written[par], 16)
                for i, (part, e, step) in enumerate(parts_dt):
                    c.after(e, step)
                    sp.dma_start(xs[par, NPROD + i].rearrange("h p d -> p h d"),
                                 tiles(part[:, XB:])).then_inc(rows_written[par], 16)
                sp.wait_ge(rows_written[par], (n - par + 2) * (WRITES * 16 // 2))
                for z in range(QUARTERS):
                    h, q0 = z * QT // Q, z * QT % Q
                    for b in range(NB):
                        row = 32 * z + (NPROD + 3) * b
                        x = xs[par, :, h].rearrange("r (g b q) d -> b r g q d", b=NB, q=Q)[b][:, :, q0:q0 + QT]
                        sp.dma_start(RM[row:row + NPROD + 3, par].rearrange("r g q d -> r g (q d)"),
                                     x.rearrange("r g q d -> r g (q d)")).then_inc(rl_loaded[par], 16)
                        x = bs[par, :, h].rearrange("r (g b q) d -> b r g q d", b=NB, q=Q)[b][:, :, q0:q0 + QT]
                        sp.dma_start(LS[row:row + NPROD, par].rearrange("r g q d -> r g (q d)"),
                                     x.rearrange("r g q d -> r g (q d)")).then_inc(rl_loaded[par], 16)

            def lora_rows(grp):
                sp.wait_ge(lora_perm, grp + 1)
                for i in range(4):
                    h, q = divmod(1 + 2 * i, Q)
                    sp.dma_start(E1[S * i:S * (i + 1), i * D:(i + 1) * D],
                                 HN[q:q + Q * (S - 1) + 1:Q, h, :]).then_inc(lora_rows_loaded, 16)
                    h, q = divmod(9 + 2 * i, Q)
                    for r in range(4):
                        row = LORA_ROWS * r + S * i
                        sp.dma_start(E2[row:row + S, i * N:(i + 1) * N],
                                     HNP[q:q + Q * (S - 1) + 1:Q, h, r, :]).then_inc(lora_rows_loaded, 16)

            spread_operands(0, 0, first=True)
            with sp.Fori(0, GROUPS) as i:
                for tau in range(UNITS_PER_GROUP):
                    m = i * UNITS_PER_GROUP + tau
                    if tau == 1:
                        lora_rows(i)
                    spread_operands(m + 1, (tau + 1) % 2)
            sp.wait_ge(rl_loaded[0], rl_count(UNITS, 0))
            sp.wait_ge(out_stored, 16 * (UNITS + 2))

        @block.gpsimd
        def _(pool):
            for t in (LS, E1, E2, O2, CS):
                nc.gpsimd.memset(t[:], 0.0).then_inc(setup_pool, 1)
            nc.gpsimd.memset(NHALF[:], -0.5).then_inc(setup_pool, 1)
            for t in (HRES, SZ, XD):
                nc.gpsimd.memset(t[:, KEPT - 1], 0.0).then_inc(setup_pool, 1)
            pool.wait_ge(setup_pool, 9)
            nc.gpsimd.sem_inc(back_sem["pool"], len(BACK_STEPS["pool"]))
            pool.wait_ge(weights_loaded, WEIGHT_LOADS * 16)

            tt, ts = nc.gpsimd.tensor_tensor, nc.gpsimd.tensor_scalar

            def gather(n, col, first=False):
                c = early(pool, "pool", n, first)
                c.after_previous("pe", "embT")
                stand(pool, "pool")
                for h in range(T2):
                    nc.gpsimd.indirect_dma_start(
                        out=EMB[:, h, :], out_offset=None, in_=table,
                        in_offset=bass.IndirectOffsetOnAxis(ap=IDX[:, col + h:col + h + 1], axis=0),
                    ).then_inc(emb_loaded, 16)

            def rstd1(n, u, first=False):
                c = early(pool, "pool", n, first)
                c.after("dve", "ag1")
                stand(pool, "pool")
                c.done(ts(VE[:, 0], MV[:, 0, :, 1], EPS, 1.0, ALU.add, ALU.mult))
                c.after("pool", "ve1")
                c.done(tt(RS[:, 0], VE[:, 0], NHALF[:], ALU.pow))

            def residual(n, u, first=False):
                c = early(pool, "pool", n, first)
                c.after("pool", "xa")
                c.done(tt(HRES[:, u % KEPT], H0[:], XA[:], ALU.add))

            def rstd2(n, u, first=False):
                c = early(pool, "pool", n, first)
                c.after("dve", "ag2")
                stand(pool, "pool")
                c.done(ts(VE[:, 1], MV[:, 1, :, 1], EPS, 1.0, ALU.add, ALU.mult))
                c.after("pool", "ve2")
                c.done(tt(RS[:, 1], VE[:, 1], NHALF[:], ALU.pow))

            def softplus_fix(n, u, first=False):
                c = late(pool, "pool", n, first)
                c.after("act", "ln")
                c.after("dve", "wl")
                c.done(tt(DW, DNA[:], DW, ALU.subtract))

            def skip_x(n, u, first=False):
                c = late(pool, "pool", n, first)
                c.after("act", "xt")
                for h in range(T2):
                    last = tt(XD[:, u % KEPT, h], PKX[:, h], DPB[:], ALU.mult)
                c.done(last)

            def split_mid(cols, name):
                def step(n, u, first=False):
                    c = late(pool, "pool", n, first)
                    c.after("act", f"hi_{name}")
                    if name == "xb":
                        c.after("pool", "xd")
                    c.done(tt(PK[:, cols], PK[:, cols], HI[:, cols], ALU.subtract))
                return step

            def split_lo(cols, name):
                def step(n, u, first=False):
                    c = late(pool, "pool", n, first)
                    c.after("act", f"mid_{name}")
                    c.after("pool", f"r1_{name}")
                    c.done(tt(LO[:, cols], PK[:, cols], MID[:, cols], ALU.subtract))
                return step

            def fill_cs(n, par, z, first=False):
                if z == 0:
                    late(pool, "pool", n, first).after("act", "cs")
                if not first:
                    pool.wait_ge(y_done, Y_CREDIT + n * TU + (z - 1) * QT)
                    pool.wait_ge(cs_filled, n * QUARTERS + z)
                stand(pool, "pool")

                def columns(q):
                    at = CS[:, z % 2, 0, 0, q:q + 1]
                    return bass.AP(tensor=at.tensor, offset=at.offset,
                                   ap=[list(at.ap[0]), [Q, S], [G * NB * Q + 1, QT]])

                h, q0 = z * QT // Q, z * QT % Q
                last = nc.gpsimd.tensor_copy(columns(q0), CT[:, par, h, :, q0:q0 + QT])
                last.then_inc(cs_filled, 1)

            def gate(m, u):
                c = back(pool, "pool", m)
                c.after("dve", "yadd")
                c.done(tt(YM[:], YG[:], SZ[:, u % KEPT], ALU.mult))

            def add_b2(m, u):
                c = back(pool, "pool", m)
                c.after("dve", "h1")
                for h in range(T2):
                    last = tt(H1B[:, h], H1[:, h], B2B[:], ALU.add)
                c.done(last)

            def rstd3(m, u):
                c = back(pool, "pool", m)
                c.after("dve", "ag")
                stand(pool, "pool")
                c.done(ts(BVE[:], BMV[:, :, 1], EPS, 1.0, ALU.add, ALU.mult))
                c.after("pool", "ve")
                c.done(tt(BRS[:], BVE[:], NHALF[:], ALU.pow))

            def norm1(n, u, first=False):
                c = early(pool, "pool", n, first)
                c.after("pool", "rs1")
                c.after_previous("pool", "cl")
                stand(pool, "pool")
                for h in range(T2):
                    last = ts(XA[:, h], H0[:, h], MV[:, 0, h, 0:1], RS[:, 0, h:h + 1], ALU.subtract, ALU.mult)
                c.done(last)

            def norm2(n, u, first=False):
                c = early(pool, "pool", n, first)
                c.after("pool", "rs2")
                c.after("pool", "hres")
                stand(pool, "pool")
                for h in range(T2):
                    last = ts(XN[:, h], XA[:, h], MV[:, 1, h, 0:1], RS[:, 1, h:h + 1], ALU.subtract, ALU.mult)
                c.done(last)

            def norm3(m, u):
                c = back(pool, "pool", m)
                c.after("pool", "rs")
                stand(pool, "pool")
                for h in range(T2):
                    last = ts(HN[:, h], H1[:, h], BMV[:, h, 0:1], BRS[:, h:h + 1], ALU.subtract, ALU.mult)
                c.done(last)

            def softplus_w(n, u, first=False):
                c = late(pool, "pool", n, first)
                c.after("act", "e")
                stand(pool, "pool")
                c.done(ts(DW, DEX, 1.0, 1.0, ALU.add, ALU.mult))

            def lora_permute(m, grp):
                c = back(pool, "pool", m)
                c.after("pool", "hn")
                stand(pool, "pool")
                for h in range(T2):
                    last = nc.gpsimd.tensor_copy(HNP[:, h], HN[:, h, :].rearrange("p (a r) -> p r a", r=4))
                last.then_inc(lora_perm, 1)

            EARLY = {26: [rstd1, norm1], 28: [rstd2, residual, norm2]}
            LATE = {13: [softplus_w, skip_x], 14: [split_mid(XB_COLS, "xb")], 16: [softplus_fix],
                    17: [split_lo(XB_COLS, "xb")], 20: [split_mid(DT_COLS, "dt")], 21: [split_lo(DT_COLS, "dt")]}
            BACK = {1: [gate], 7: [rstd3, norm3], 8: [add_b2]}
            FILL = {3: 1, 11: 2, 19: 3, 27: 0}
            GATHER, PERMUTE = 12, 10

            pool.dma_start(IDX[:], idx[0]).then_inc(idx_loaded, 16)
            pool.wait_ge(idx_loaded, 16)
            gather(0, 0, first=True)
            for steps in (EARLY, LATE):
                for t in range(TU):
                    for step in steps.get(t, []):
                        step(0, 0, first=True)
            fill_cs(0, 0, 0, first=True)
            gather(1, T2)
            for t in range(TU):
                for step in EARLY.get(t, []):
                    step(1, 1)
            with pool.Fori(0, GROUPS) as i:
                pool.wait_ge(emb_loaded, i * (UNITS_PER_GROUP * T2 * 16) + 16 * 2 * T2)
                pool.dma_start(IDX[:], idx[bass.ds(i + 1, 1)].rearrange("a p c -> (a p) c")).then_inc(idx_loaded, 16)
                pool.wait_ge(idx_loaded, i * 16 + 32)
                for tau in range(UNITS_PER_GROUP):
                    m = i * UNITS_PER_GROUP + tau
                    for t in range(TU):
                        for step in BACK.get(t, []):
                            step(m, tau - 1)
                        if tau == 1 and t == PERMUTE:
                            lora_permute(m, i)
                        for step in LATE.get(t, []):
                            step(m + 1, tau + 1)
                        if t == GATHER:
                            gather(m + 2, T2 * tau)
                        for step in EARLY.get(t, []):
                            step(m + 2, tau + 2)
                        if t in FILL:
                            if FILL[t]:
                                fill_cs(m, tau % 2, FILL[t])
                            else:
                                fill_cs(m + 1, (tau + 1) % 2, 0)
            for t in range(TU):
                for step in BACK.get(t, []):
                    step(UNITS, -1)

        @block.scalar
        def _(act):
            f = nc.scalar.activation
            act.wait_ge(weights_loaded, WEIGHT_LOADS * 16)
            f(ACOL[:, 1:2], ACOL[:, 0:1], ACT.Exp).then_inc(setup_act, 1)
            act.wait_ge(setup_act, 1)
            f(ACOL[:, 0:1], ACOL[:, 1:2], ACT.Copy, scale=-1.0).then_inc(setup_act, 1)
            act.wait_ge(setup_act, 2)
            act.wait_ge(setup_pe, 2)
            f(XBIAS[:], FA[:, 0:K2], ACT.Copy).then_inc(setup_act, 1)
            f(ZBIAS[:], FB[:, 0:D], ACT.Copy).then_inc(setup_act, 1)
            act.wait_ge(setup_act, 4)
            nc.scalar.sem_inc(a_ready, A_CREDIT)
            nc.scalar.sem_inc(back_sem["act"], len(BACK_STEPS["act"]))

            def embT(n, u, first=False):
                c = early(act, "act", n, first)
                c.after("pe", "embT")
                c.done(f(EMBT, FA[0:E, 0:TOK], ACT.Copy))

            def h0(n, u, first=False):
                c = early(act, "act", n, first)
                c.after("pe", "h0")
                c.after_previous("dve", "dt")
                c.done(f(H0[:], FB[:, :], ACT.Copy))

            def xnT(n, u, first=False):
                c = late(act, "act", n, first)
                c.after("pe", "xnT")
                c.done(f(XNT[:], FA[:, :], ACT.Copy))

            def xm(n, u, first=False):
                c = late(act, "act", n, first)
                c.after("pe", "xm")
                c.after("dve", "carry")
                for k in range(K2):
                    last = f(by_token(XM[:, k, :, TAPS - 1:]),
                             FB[:, k * TOK:(k + 1) * TOK].rearrange("p (h s q) -> p h s q", h=T2, q=Q),
                             ACT.Identity, bias=XBIAS[:, k:k + 1])
                c.done(last)

            def silu(n, u, first=False):
                c = late(act, "act", n, first)
                c.after("dve", "z")
                for k in range(K2):
                    last = f(XCT[:, k, :].rearrange("p (h s q) -> p h s q", h=T2, q=Q),
                             by_token(CV[1][:, k]), ACT.Silu)
                c.done(last)
                c.done(f(SZ[:, u % KEPT], ZT[:], ACT.Silu))

            def softplus_exp(n, u, first=False):
                c = late(act, "act", n, first)
                c.after("dve", "na")
                c.done(f(DEX, DNA[:], ACT.Exp))

            def softplus_ln(n, u, first=False):
                c = late(act, "act", n, first)
                c.after("pool", "w")
                c.done(f(DNA[:], DW, ACT.Ln))

            def bc(n, u, par, first=False):
                c = late(act, "act", n, first)
                c.after("pe", "bc")
                c.after_previous("pool", "lo_xb")
                for b in range(NB):
                    last = f(PKB[:, :, b, :], FA[:, 0:T2 * N].rearrange("p (h n) -> p h n", h=T2), ACT.Identity,
                             scale=OWN[:, b:b + 1])
                c.done(last)
                for b in range(NB):
                    last = f(CT[:, par].rearrange("p h (g b) q -> p (h g) b q", b=NB)[:, :, b, :],
                             FA[:, 128:128 + TOK].rearrange("p (x b q) -> p x b q", b=NB, q=Q)[:, :, b, :],
                             ACT.Identity, scale=HALF[:, b:b + 1])
                c.done(last)

            def xt(n, u, first=False):
                c = late(act, "act", n, first)
                c.after("pe", "xt")
                c.done(f(PK[:, 0:XW], FB[:, :], ACT.Copy))

            def split_hi(cols, name):
                def step(n, u, par, first=False):
                    c = late(act, "act", n, first)
                    if name == "xb":
                        c.after("act", "xt")
                        if not first:
                            act.wait_ge(rows_written[1 - par], (n - 1 - (1 - par) + 2) * (WRITES * 16 // 2))
                    else:
                        c.after("dve", "dt")
                    c.done(f(HI[:, cols], PK[:, cols], ACT.Copy))
                return step

            def split_mid(cols, name):
                def step(n, u, par, first=False):
                    c = late(act, "act", n, first)
                    c.after("pool", f"r1_{name}")
                    c.done(f(MID[:, cols], PK[:, cols], ACT.Copy))
                return step

            def yT(m, u):
                c = back(act, "act", m)
                c.after("pe", "yT")
                c.done(f(YT[:], BA[:, :], ACT.Copy))

            def hnT(m, u):
                c = back(act, "act", m)
                c.after("pe", "hnT")
                c.done(f(HNT[:], BA[:, :], ACT.Copy))

            def hidden(k):
                def step(m, u):
                    c = back(act, "act", m)
                    c.after("pe", f"hid{k}")
                    c.done(f(HH[:, k, :], (BA, FB)[k % 2][:, 0:TOK], ACT.Identity, bias=B1C[:, k:k + 1]))
                return step

            def gelu(m, u):
                c = back(act, "act", m)
                c.after("act", f"hid{HC - 1}")
                c.done(f(HH[:], HH[:], ACT.Gelu))

            def store(m):
                act.wait_ge(back_sem["dve"], back_count("dve", "out", m - 1))
                slot = out[m] if m is UNITS else out[bass.ds(m, 1)].rearrange("a p h d -> (a p) h d")
                act.dma_start(slot, OUT[:, :, :]).then_inc(out_stored, 16)

            EARLY = {23: [embT], 26: [h0]}
            LATE = {0: [xnT], 3: [xm], 8: [silu], 11: [bc], 12: [softplus_exp], 13: [xt, split_hi(XB_COLS, "xb")],
                    15: [softplus_ln], 16: [split_mid(XB_COLS, "xb")], 19: [split_hi(DT_COLS, "dt")],
                    21: [split_mid(DT_COLS, "dt")]}
            BACK = {4: [yT], 12: [hnT]} | {16 + k: [hidden(k)] for k in range(HC)} | {24: [gelu]}
            STORE = 3

            def run(table, n, u, par, t, first=False):
                for step in table.get(t, []):
                    if step in (embT, h0, xnT, xm, silu, softplus_exp, softplus_ln, xt):
                        step(n, u, first)
                    else:
                        step(n, u, par, first)

            def scan_step(m, t):
                T = m * TU + t
                for e in range(HALVES):
                    act.wait_ge(dt_ready, HALVES * T + e + 1)
                    act.wait_ge(v_done, HALVES * T + e + 1)
                    f(AR[:, t % A_RING, e], DT[e][:, :], ACT.Exp, scale=ACOL[:, 0:1]).then_inc(a_ready, 1)

            for n, table in ((0, EARLY), (0, LATE), (1, EARLY)):
                for t in range(TU):
                    run(table, n, n, n, t, first=(n == 0))
            with act.Fori(0, GROUPS) as i:
                for tau in range(UNITS_PER_GROUP):
                    m = i * UNITS_PER_GROUP + tau
                    for t in range(TU):
                        scan_step(m, t)
                        if t == STORE:
                            store(m)
                        for step in BACK.get(t, []):
                            step(m, tau - 1)
                        run(LATE, m + 1, tau + 1, (tau + 1) % 2, t)
                        run(EARLY, m + 2, tau + 2, tau % 2, t)
            scan_step(UNITS, 0)
            store(UNITS)
            for t in range(TU):
                for step in BACK.get(t, []):
                    step(UNITS, -1)
            act.wait_ge(back_sem["dve"], back_count("dve", "out", UNITS))
            act.dma_start(out[UNITS + 1], OUT[:, :, :]).then_inc(out_stored, 16)

        @block.vector
        def _(dve):
            tt, ts, stt = nc.vector.tensor_tensor, nc.vector.tensor_scalar, nc.vector.scalar_tensor_tensor
            nc.vector.memset(RM[:], 0.0).then_inc(setup_dve, 1)
            nc.vector.memset(V[:], 0.0).then_inc(setup_dve, 1)
            nc.vector.memset(HR[:], 0.0).then_inc(setup_dve, 1)
            nc.vector.memset(Y[:, :], 0.0).then_inc(setup_dve, 1)
            nc.vector.memset(O1[:], 0.0).then_inc(setup_dve, 1)
            nc.vector.memset(XM[:], 0.0).then_inc(setup_dve, 1)
            nc.vector.memset(LNBW, 1.0).then_inc(setup_dve, 1)
            nc.vector.memset(OUT[:], 0.0).then_inc(setup_dve, 1)
            dve.wait_ge(setup_dve, 8)
            dve.wait_ge(weights_loaded, WEIGHT_LOADS * 16)
            for k in range(K2):
                last = ts(LNBW[:, k, :], LNBW[:, k, :], LNB[:, k:k + 1], None, ALU.mult)
            last.then_inc(setup_dve, 1)
            dve.wait_ge(setup_pe, 2)
            for k in range(K2):
                last = ts(WIN[:, k, :], WIN[:, k, :], LNG[:, k:k + 1], None, ALU.mult)
            last.then_inc(setup_dve, 1)
            dve.wait_ge(setup_dve, 10)
            dve.wait_ge(setup_act, 4)
            dve.wait_ge(setup_pool, 9)
            nc.vector.sem_inc(v_done, V_CREDIT)
            nc.vector.sem_inc(h_done, H_CREDIT)
            nc.vector.sem_inc(lora_cols, 1)
            nc.vector.sem_inc(back_sem["dve"], len(BACK_STEPS["dve"]))

            def carry(n, u, first=False):
                c = late(dve, "dve", n, first)
                c.after_previous("dve", "cv3")
                c.after_previous("act", "xm")
                if u % UNITS_PER_GROUP == 0:
                    c.done(nc.vector.memset(XM[:, :, :, 0:TAPS - 1], 0.0))
                else:
                    c.done(nc.vector.tensor_copy(XM[:, :, :, 0:TAPS - 1], XM[:, :, :, TU:TU + TAPS - 1]))

            def stats(c, src, k, st, ag):
                for h in range(T2):
                    last = nc.vector.bn_stats(ST[:, k, h, :], src[:, h, :])
                c.done(last)
                c.after("dve", st)
                stand(dve, "dve")
                for h in range(T2):
                    last = nc.vector.bn_aggr(MV[:, k, h, :], ST[:, k, h, :])
                c.done(last)

            def stats1(n, u, first=False):
                c = early(dve, "dve", n, first)
                c.after("act", "h0")
                stats(c, H0, 0, "st1", "ag1")

            def stats2(n, u, first=False):
                c = early(dve, "dve", n, first)
                c.after("pool", "xa")
                stats(c, XA, 1, "st2", "ag2")

            def z(n, u, first=False):
                c = late(dve, "dve", n, first)
                c.after("pe", "z")
                c.after_previous("act", "silu_z")
                for h in range(T2):
                    last = tt(ZT[:, h], FA[:, h * D:(h + 1) * D], ZBIAS[:], ALU.add)
                c.done(last)

            def conv(part):
                def step(n, u, first=False):
                    c = late(dve, "dve", n, first)
                    c.after("act", "xm")
                    c.after_previous("dve", "dt")
                    for tap in (part,):
                        if tap:
                            c.after("dve", f"cv{tap - 1}")
                        at = TAPS - 1 - tap
                        for k in range(K2):
                            x = XM[:, k, :, at:at + TU]
                            if tap == 0:
                                last = ts(CV[0][:, k], x, CONVW[:, k, at:at + 1], CONVB[:, k:k + 1], ALU.mult, ALU.add)
                            else:
                                last = stt(CV[tap % 2][:, k], x, CONVW[:, k, at:at + 1], CV[1 - tap % 2][:, k],
                                           ALU.mult, ALU.add)
                        c.done(last)
                return step

            def dt_pre(n, u, first=False):
                c = late(dve, "dve", n, first)
                c.after("pe", "dt")
                for h in range(T2):
                    last = tt(DTX[:, h], FB[:, h * D:(h + 1) * D], BDTB[:], ALU.add)
                c.done(last)
                c.after("dve", "dtx")
                c.done(stt(DNA[:], DTX[:], -1.0, DTX[:], ALU.mult, ALU.min))

            def softplus_lost(n, u, first=False):
                c = late(dve, "dve", n, first)
                c.after("act", "ln")
                c.done(stt(DW, DW, 1.0, DEX, ALU.subtract, ALU.subtract))

            def dt_post(n, u, first=False):
                c = late(dve, "dve", n, first)
                c.after("pool", "cl")
                c.done(stt(PKDT, DTX[:], 0.0, DW, ALU.max, ALU.add))

            def y_add(m, u):
                c = back(dve, "dve", m)
                dve.wait_ge(y_done, Y_CREDIT + m * TU)
                c.done(tt(YG[:], tiles(Y[:, :]), XD[:, u % KEPT], ALU.add))

            def h1(m, u):
                c = back(dve, "dve", m)
                c.after("pe", "wo")
                dve.wait_ge(out_stored, (m + 1) * 16)
                c.done(tt(H1[:], tiles(BA[:, :]), HRES[:, u % KEPT], ALU.add))
                c.after("dve", "h1")
                for h in range(T2):
                    last = nc.vector.bn_stats(BST[:, h, :], H1[:, h, :])
                c.done(last)
                c.after("dve", "st")
                stand(dve, "dve")
                for h in range(T2):
                    last = nc.vector.bn_aggr(BMV[:, h, :], BST[:, h, :])
                c.done(last)

            def lora_columns(m, grp):
                c = back(dve, "dve", m)
                c.after("act", "hnT")
                c.after_previous("pe", "q")
                for i in range(4):
                    for dst, t in ((O1, 2 + 2 * i), (O2, 10 + 2 * i)):
                        h, q = divmod(t, Q)
                        last = nc.vector.tensor_copy(
                            dst[:, :, S * i:S * (i + 1)],
                            HNT[:, :, h * 128 + q:h * 128 + q + Q * (S - 1) + 1:Q])
                last.then_inc(lora_cols, 1)

            def sm(m, u):
                c = back(dve, "dve", m)
                c.after("pe", "s")
                c.done(stt(SM[:], BA[0:LORA_ROWS, 0:TOK], SCL[0:LORA_ROWS, 0:1], MASKQ[0:LORA_ROWS, :], ALU.mult, ALU.mult))

            def qm(m, u):
                c = back(dve, "dve", m)
                c.after("pe", "q")
                c.done(stt(QM, FA[:, 0:TOK], SCL[:, 0:1], MASKQ[:], ALU.mult, ALU.mult))

            def out_add(m, u):
                c = back(dve, "dve", m)
                c.after("pe", "out")
                c.after("pool", "h1b")
                c.done(tt(OUT[:], tiles(BA[:, :]), H1B[:], ALU.add))

            EARLY = {26: [stats1], 28: [stats2]}
            LATE = {0: [carry], 3: [conv(0)], 4: [conv(1)], 5: [conv(2)], 6: [conv(3), z], 10: [dt_pre],
                    16: [softplus_lost], 18: [dt_post]}
            BACK = {0: [y_add], 7: [h1], 13: [sm], 26: [qm], 31: [out_add]}
            COLUMNS = 12

            def scan_step(m, t, fresh):
                T = m * TU + t
                for e in range(HALVES):
                    dve.wait_ge(a_ready, A_CREDIT + HALVES * T + e + 1)
                    dve.wait_ge(h_done, H_CREDIT + HALVES * (T - 1) + e + 1)
                    if fresh:
                        last = nc.vector.memset(V[:, e], 0.0)
                    else:
                        last = tt(V[:, e], AR[:, t % A_RING, e], HR[:, (t - 1) % H_RING, e], ALU.mult)
                    last.then_inc(v_done, 1)
                dve.wait_ge(y_done, T + 1)
                for e in range(HALVES):
                    dve.wait_ge(v_done, V_CREDIT + HALVES * T + e + 1)
                    dve.wait_ge(u_ready, HALVES * T + e + 1)
                    tt(HR[:, t % H_RING, e], V[:, e], U[e][:, :], ALU.add).then_inc(h_done, 1)

            for n, table in ((0, EARLY), (0, LATE), (1, EARLY)):
                for t in range(TU):
                    for step in table.get(t, []):
                        step(n, n, n == 0)
            with dve.Fori(0, GROUPS) as i:
                for tau in range(UNITS_PER_GROUP):
                    m = i * UNITS_PER_GROUP + tau
                    for t in range(TU):
                        scan_step(m, t, tau == 0 and t == 0)
                        for step in BACK.get(t, []):
                            step(m, tau - 1)
                        if tau == 1 and t == COLUMNS:
                            lora_columns(m, i)
                        for step in LATE.get(t, []):
                            step(m + 1, tau + 1)
                        for step in EARLY.get(t, []):
                            step(m + 2, tau + 2)
            for t in range(TU):
                for step in BACK.get(t, []):
                    step(UNITS, -1)

        @block.tensor
        def _(pe):
            mm = nc.tensor.matmul
            pe.wait_ge(weights_loaded, WEIGHT_LOADS * 16)
            for e in range(K2):
                for k in range(K2):
                    last = mm(FA[:, e:e + 1], WIN[:, k, e * 128:(e + 1) * 128], LNB[:, k:k + 1],
                              start=(k == 0), stop=(k == K2 - 1))
            last.then_inc(setup_pe, 1)
            pe.wait_ge(setup_dve, 9)
            for k in range(K2):
                last = mm(FB[:, 0:D], LNBW[:, k, :], WIN[:, k, D:2 * D], start=(k == 0), stop=(k == K2 - 1))
            last.then_inc(setup_pe, 1)
            pe.wait_ge(setup_dve, 10)
            pe.wait_ge(setup_act, 4)
            pe.wait_ge(setup_pool, 9)
            nc.tensor.sem_inc(y_done, Y_CREDIT)
            nc.tensor.sem_inc(back_sem["pe"], len(BACK_STEPS["pe"]))

            def embT(n, first=False, slot=None):
                c = early(pe, "pe", n, first)
                pe.wait_ge(emb_loaded, (n + 1) * (16 * T2))
                c.after_previous("act", "cs")
                stand(pe, "pe")
                for h in range(T2):
                    last = nc.tensor.transpose(FA[0:E, h * 128:(h + 1) * 128], EMB[:, h, :], IDENT[:])
                c.done(last)

            def h0(n, first=False, slot=None):
                c = early(pe, "pe", n, first)
                if slot is not None:
                    back(pe, "pe", slot).after("act", f"hid{HC - 1}")
                c.after("act", "embT")
                c.after_previous("act", "xt")
                for h in range(T2):
                    last = mm(FB[:, h * D:(h + 1) * D], EMBT[:, h * 128:(h + 1) * 128], PROJ[:],
                              start=True, stop=True)
                c.done(last)

            def transposed(dst, src):
                for k in range(K2):
                    for h in range(T2):
                        last = nc.tensor.transpose(dst[:, k * TOK + h * 128:k * TOK + (h + 1) * 128],
                                                   src[:, h, k * 128:(k + 1) * 128], IDENT[:])
                return last

            def xnT(n, first=False, slot=None):
                c = early(pe, "pe", n, first)
                if slot is not None:
                    back(pe, "pe", slot).after("dve", "qm")
                c.after("pool", "xn")
                c.after("act", "embT")
                c.done(transposed(FA, XN))

            def xm(part):
                def step(n, first=False):
                    c = late(pe, "pe", n, first)
                    if part == 0:
                        c.after("act", "xnT")
                        c.after("act", "h0")
                    for k in range(K2):
                        last = mm(FB[:, part * TOK:(part + 1) * TOK], WIN[:, k, part * 128:(part + 1) * 128],
                                  XNT[:, k, :], start=(k == 0), stop=(k == K2 - 1))
                    if part == K2 - 1:
                        c.done(last)
                return step

            def tile_product(dst, width, h, lhs, rhs):
                for k in range(K2):
                    last = mm(dst[:, h * width:(h + 1) * width], lhs[:, k, h * 128:(h + 1) * 128], rhs[:, k],
                              start=(k == 0), stop=(k == K2 - 1))
                return last

            def z(h):
                def step(n, first=False):
                    c = late(pe, "pe", n, first)
                    if h == 0:
                        c.after("act", "xnT")
                    last = tile_product(FA, D, h, XNT, WIN[:, :, D:2 * D])
                    if h == T2 - 1:
                        c.done(last)
                return step

            def dt(h):
                def step(n, first=False):
                    c = late(pe, "pe", n, first)
                    if h == 0:
                        c.after("act", "silu_x")
                        c.after("act", "xm")
                    last = tile_product(FB, D, h, XCT, WDTB[:, :, 0:D])
                    if h == T2 - 1:
                        c.done(last)
                return step

            def bc(n, first=False):
                c = late(pe, "pe", n, first)
                c.after("act", "silu_x")
                c.after("dve", "z")
                for h in range(T2):
                    tile_product(FA, N, h, XCT, WDTB[:, :, D:D + N])
                for k in range(K2):
                    last = mm(FA[:, 128:128 + TOK], WC2[:, k, :], XCT[:, k, :], start=(k == 0), stop=(k == K2 - 1))
                c.done(last)

            def xt(n, first=False):
                c = late(pe, "pe", n, first)
                c.after("dve", "dtx")
                for h in range(T2):
                    for k in range(K2):
                        last = nc.tensor.transpose(FB[:, h * D + k * 128:h * D + (k + 1) * 128],
                                                   XCT[:, k, h * 128:(h + 1) * 128], IDENT[:])
                c.done(last)

            def yT(m, grp, fronts=True):
                c = back(pe, "pe", m)
                c.after("pool", "ymul")
                c.after_previous("dve", "out")
                c.done(transposed(BA, YM))

            def wo(h):
                def step(m, grp, fronts=True):
                    c = back(pe, "pe", m)
                    c.after("act", "yT")
                    last = tile_product(BA, D, h, YT, WOUT[:, :, :])
                    if h == T2 - 1:
                        c.done(last)
                return step

            def hnT(m, grp, fronts=True):
                c = back(pe, "pe", m)
                c.after("pool", "hn")
                c.done(transposed(BA, HN))

            def s(m, grp, fronts=True):
                c = back(pe, "pe", m)
                c.after("act", "hnT")
                pe.wait_ge(lora_cols, grp + 1)
                for k in range(K2):
                    last = mm(BA[0:LORA_ROWS, 0:TOK], O1[:, k, :], HNT[:, k, :], start=(k == 0), stop=(k == K2 - 1))
                c.done(last)

            def hidden(chunk):
                def step(m, grp, fronts=True):
                    c = back(pe, "pe", m)
                    if chunk == 0:
                        c.after("dve", "sm")
                        pe.wait_ge(lora_rows_loaded, grp * (4 * 5 * 16) + 16)
                    elif chunk >= 2:
                        c.after("act", f"hid{chunk - 2}")
                    elif fronts:
                        late(pe, "pe", m + 1).after("act", "xt")
                    dst, col = (BA, FB)[chunk % 2][:, 0:TOK], chunk * 128
                    for k in range(K2):
                        mm(dst, W1[:, k, col:col + 128], HNT[:, k, :], start=(k == 0), stop=False)
                    c.done(mm(dst, E1[:, col:col + 128], SM[:], start=False, stop=True))
                return step

            def q(m, grp, fronts=True):
                c = back(pe, "pe", m)
                c.after("act", "gelu")
                if fronts:
                    early(pe, "pe", m + 2).after("act", "embT")
                for k in range(K2):
                    for r in range(4):
                        last = mm(FA[32 * r:32 * r + 32, 0:TOK], O2[:, k, :], HH[:, K2 * r + k, :],
                                  start=(k == 0), stop=(k == K2 - 1), tile_position=(0, 32 * r))
                c.done(last)

            def out_mm(h, k0, k1):
                def step(m, grp, fronts=True):
                    c = back(pe, "pe", m)
                    if h == T2 - 1 and k0 == 0:
                        c.after("act", "gelu")
                    dst = BA[:, h * D:(h + 1) * D]
                    for k in range(k0, k1):
                        mm(dst, HH[:, k, h * 128:(h + 1) * 128], W2[:, k, :], start=(k == 0), stop=False)
                    if k1 == HC:
                        c.after("dve", "qm")
                        last = mm(dst, QM[:, h * 128:(h + 1) * 128], E2[:], start=False, stop=True)
                        if h == 0:
                            c.done(last)
                return step

            EARLY = {21: [embT], 24: [h0], 31: [xnT]}
            LATE = {0: [xm(0)], 1: [xm(1)], 3: [z(0)], 4: [z(1)], 7: [dt(0)], 8: [dt(1)], 9: [bc], 11: [xt]}
            BACK = {2: [yT], 5: [wo(0)], 6: [wo(1)], 10: [hnT], 12: [s], 25: [q], 26: [out_mm(1, 0, 3)], 27: [out_mm(1, 3, 6)],
                    28: [out_mm(1, 6, 8)], 29: [out_mm(0, 0, 4)], 30: [out_mm(0, 4, 8)]}
            BACK |= {14 + c: [hidden(c)] for c in range(HC)}

            def scan_dt(m, tau, t):
                T = m * TU + t
                par, local = (tau + t // TU) % 2, t % TU
                if local == 0:
                    pe.wait_ge(rl_loaded[par], rl_count(m + t // TU, par))
                for e in range(HALVES):
                    pe.wait_ge(a_ready, HALVES * T + e + 1)
                    for g in range(PH):
                        last = mm(DT[e][:, g * D:(g + 1) * D], SEL[:, local // QT, :],
                                  RM[:, par, PH * e + g, local % QT, :], start=True, stop=True)
                    last.then_inc(dt_ready, 1)

            def scan_u(m, par, t):
                T = m * TU + t
                rows = slice(32 * (t // QT), 32 * (t // QT) + NROW)
                for e in range(HALVES):
                    pe.wait_ge(h_done, HALVES * T + e + 1)
                    for g in range(PH):
                        last = mm(U[e][:, g * D:(g + 1) * D], LS[rows, par, PH * e + g, t % QT, :],
                                  RM[rows, par, PH * e + g, t % QT, :],
                                  start=True, stop=True, tile_position=(rows.start, 0))
                    last.then_inc(u_ready, 1)

            def scan_y(m, t, slot):
                pe.wait_ge(h_done, H_CREDIT + HALVES * (m * TU + t + 1))
                if t == 0:
                    pe.wait_ge(back_sem["dve"], back_count("dve", "yadd", slot))
                if t % QT == 0:
                    pe.wait_ge(cs_filled, m * QUARTERS + t // QT + 1)
                h = t // Q
                for g in range(G):
                    last = mm(Y[32 * g:32 * g + 32, h * D:(h + 1) * D], CS[:, t // QT % 2, t % QT, g, :],
                              HR[:, t % H_RING, g // PH, g % PH * D:(g % PH + 1) * D],
                              start=(t == 0), stop=(t % Q == Q - 1),
                              tile_position=(0, 32 * g), skip_group_check=True)
                last.then_inc(y_done, 1)

            for n, table in ((0, EARLY), (0, LATE), (1, EARLY)):
                for t in range(TU):
                    for step in table.get(t, []):
                        step(n, n == 0)
            for t in range(AHEAD):
                scan_dt(0, 0, t)
            with pe.Fori(0, GROUPS) as i:
                for tau in range(UNITS_PER_GROUP):
                    m = i * UNITS_PER_GROUP + tau
                    grp = i if tau == 0 else i + 1
                    for t in range(TU):
                        scan_u(m, tau % 2, t)
                        if t:
                            scan_y(m, t - 1, m)
                        elif tau:
                            scan_y(m - 1, TU - 1, m)
                        for step in BACK.get(t, []):
                            step(m, grp)
                        for step in LATE.get(t, []):
                            step(m + 1)
                        for step in EARLY.get(t, []):
                            step(m + 2, slot=m)
                        scan_dt(m, tau, t + AHEAD)
                    if tau == UNITS_PER_GROUP - 1:
                        scan_y(m, TU - 1, m)
            for t in range(TU):
                for step in BACK.get(t, []):
                    step(UNITS, GROUPS, fronts=False)


def program(nc, args):
    build(nc, *args)


def kernel(x, L0_tok_emb_table, L0_tok_proj_w, L0_attn_ln_g, L0_attn_ln_b, L0_attn_W_in, L0_attn_conv_w,
           L0_attn_conv_b, L0_attn_A_log, L0_attn_Dp, L0_attn_W_dt, L0_attn_b_dt, L0_attn_W_B, L0_attn_W_C,
           L0_attn_W_out, L0_ffn_W1, L0_ffn_b1, L0_ffn_W2, L0_ffn_b2, L0_ffn_scale):
    import ml_dtypes
    import numpy as np
    import concourse.bacc as bacc
    from concourse.bass_utils import run_bass_kernel_spmd

    def arr(a):
        return np.ascontiguousarray(np.asarray(a))

    def by_rows(w):
        w = np.asarray(w)
        return arr(w.T.reshape(-1, 128, w.shape[0]).transpose(1, 0, 2))

    def by_cols(v):
        return arr(np.asarray(v).reshape(-1, 128).T)

    xi = np.asarray(x).reshape(GROUPS, S, UNITS_PER_GROUP, T2, Q).transpose(0, 2, 1, 4, 3)
    xi = xi.reshape(UNITS, 128, T2)
    idx = np.zeros((GROUPS + 1, 128, UNITS_PER_GROUP, T2), xi.dtype)
    idx[0, :, 0:2] = xi[0:2].transpose(1, 0, 2)
    for i in range(GROUPS):
        for tau in range(UNITS_PER_GROUP):
            if i * UNITS_PER_GROUP + tau + 2 < UNITS:
                idx[i + 1, :, tau] = xi[i * UNITS_PER_GROUP + tau + 2]
    idx = idx.reshape(GROUPS + 1, 128, UNITS_PER_GROUP * T2)

    sel = np.zeros((128, QUARTERS, 128), ml_dtypes.bfloat16)
    for z in range(QUARTERS):
        for b in range(NB):
            row = 32 * z + (NPROD + 3) * b + NPROD
            sel[row:row + 3, z, N * b:N * b + N] = 1
    half = np.repeat(np.eye(NB, dtype=np.float32), N, axis=0)
    own = np.tile(np.repeat(np.eye(NB, dtype=np.float32), Q, axis=0), (G, 1))
    maskq = np.zeros((4 * 4, S, T2, S, Q), np.float32)
    for sq in range(S):
        maskq[:, sq, :, sq] = 1
    maskq = maskq.reshape(128, TOK)

    wc = np.asarray(L0_attn_W_C)
    alog = np.asarray(L0_attn_A_log)
    ins = {
        "idx": idx, "table": arr(L0_tok_emb_table), "proj": arr(np.asarray(L0_tok_proj_w).T),
        "win": by_rows(L0_attn_W_in),
        "wdtb": by_rows(np.concatenate([np.asarray(L0_attn_W_dt), np.asarray(L0_attn_W_B)])),
        "wc2": by_rows(np.concatenate([wc, wc])), "wout": by_rows(L0_attn_W_out),
        "w1": by_rows(L0_ffn_W1), "w2": by_rows(L0_ffn_W2),
        "lng": by_cols(L0_attn_ln_g), "lnb": by_cols(L0_attn_ln_b),
        "convw": arr(np.asarray(L0_attn_conv_w).reshape(K2, 128, TAPS).transpose(1, 0, 2)),
        "convb": by_cols(L0_attn_conv_b), "alog": arr(np.concatenate([alog, alog]).reshape(128, 1)),
        "dp": arr(L0_attn_Dp).reshape(1, D), "bdt": arr(L0_attn_b_dt).reshape(1, D),
        "b1": by_cols(L0_ffn_b1), "b2": arr(L0_ffn_b2).reshape(1, D),
        "scale": arr(L0_ffn_scale).reshape(1, 1),
        "ident": np.eye(128, dtype=np.float32), "sel": sel, "own": own, "half": half, "maskq": maskq,
    }
    nc = bacc.Bacc("TRN2", target_bir_lowering=False, num_devices=1)
    args = [nc.dram_tensor(f"in_{k}", a.shape, mybir.dt.from_np(a.dtype), kind="ExternalInput").ap()
            for k, a in ins.items()]
    args.append(nc.dram_tensor("rows_x", (2, NPROD + 3, T2, 128, D), BF16, kind="Internal").ap())
    args.append(nc.dram_tensor("rows_b", (2, NPROD, T2, 128, NB * N), BF16, kind="Internal").ap())
    args.append(nc.dram_tensor("out", (UNITS + 2, 128, T2, D), F32, kind="ExternalOutput").ap())
    program(nc, args)
    r = run_bass_kernel_spmd(nc, [{f"in_{k}": a for k, a in ins.items()}], core_ids=[0])
    o = r.results[0]["out"][2:].reshape(GROUPS, UNITS_PER_GROUP, S, Q, T2, D)
    return arr(o.transpose(0, 2, 1, 4, 3, 5)).reshape(BATCH, SEQ, D)
```
